# Optimizing a Trainium2 kernel written in Bass

```python
import numpy as np
import jax
import jax.numpy as jnp

def _softmax(x, axis=-1):
    return jax.nn.softmax(x, axis=axis)

def _gelu(x):
    return jax.nn.gelu(x, approximate=True)

def _silu(x):
    return jax.nn.silu(x)

def _sigmoid(x):
    return jax.nn.sigmoid(x)

def _layernorm(x, axis=-1, eps=1e-05):
    m = jnp.mean(x, axis=axis, keepdims=True)
    v = jnp.var(x, axis=axis, keepdims=True)
    return (x - m) / jnp.sqrt(v + eps)

def _scatter_add(tgt, idx, src, axis=0):
    return tgt.at[idx].add(src)

def _segment_sum(src, seg, n):
    return jax.ops.segment_sum(src, seg, n)
kernel_name = 'mk_rec_standalone_d1_rec_r8_64eb30'

def setup_inputs(seed: int=0):
    np.random.seed(seed)
    _w = jnp.asarray

    def _rec_inputs():
        import jax
        import jax.numpy as jnp
        _rk = jax.random.key(seed)
        r_lS_o = jax.random.randint(jax.random.fold_in(_rk, 1), (26, 4096), 0, 4096, jnp.int32)
        r_lS_i = jnp.stack([jax.random.randint(jax.random.fold_in(jax.random.fold_in(_rk, 2), 0), (4096,), 2, 6250, jnp.int32), jax.random.randint(jax.random.fold_in(jax.random.fold_in(_rk, 2), 1), (4096,), 0, 49998, jnp.int32), jax.random.randint(jax.random.fold_in(jax.random.fold_in(_rk, 2), 2), (4096,), 0, 49999, jnp.int32), jax.random.randint(jax.random.fold_in(jax.random.fold_in(_rk, 2), 3), (4096,), 0, 6250, jnp.int32), jax.random.randint(jax.random.fold_in(jax.random.fold_in(_rk, 2), 4), (4096,), 0, 49999, jnp.int32), jax.random.randint(jax.random.fold_in(jax.random.fold_in(_rk, 2), 5), (4096,), 0, 6250, jnp.int32), jax.random.randint(jax.random.fold_in(jax.random.fold_in(_rk, 2), 6), (4096,), 0, 6250, jnp.int32), jax.random.randint(jax.random.fold_in(jax.random.fold_in(_rk, 2), 7), (4096,), 1, 49998, jnp.int32), jax.random.randint(jax.random.fold_in(jax.random.fold_in(_rk, 2), 8), (4096,), 0, 49991, jnp.int32), jax.random.randint(jax.random.fold_in(jax.random.fold_in(_rk, 2), 9), (4096,), 0, 49998, jnp.int32), jax.random.randint(jax.random.fold_in(jax.random.fold_in(_rk, 2), 10), (4096,), 2, 49999, jnp.int32), jax.random.randint(jax.random.fold_in(jax.random.fold_in(_rk, 2), 11), (4096,), 1, 49998, jnp.int32), jax.random.randint(jax.random.fold_in(jax.random.fold_in(_rk, 2), 12), (4096,), 0, 6250, jnp.int32), jax.random.randint(jax.random.fold_in(jax.random.fold_in(_rk, 2), 13), (4096,), 2, 49998, jnp.int32), jax.random.randint(jax.random.fold_in(jax.random.fold_in(_rk, 2), 14), (4096,), 1, 6250, jnp.int32), jax.random.randint(jax.random.fold_in(jax.random.fold_in(_rk, 2), 15), (4096,), 0, 49998, jnp.int32), jax.random.randint(jax.random.fold_in(jax.random.fold_in(_rk, 2), 16), (4096,), 0, 6250, jnp.int32), jax.random.randint(jax.random.fold_in(jax.random.fold_in(_rk, 2), 17), (4096,), 0, 49997, jnp.int32), jax.random.randint(jax.random.fold_in(jax.random.fold_in(_rk, 2), 18), (4096,), 1, 6250, jnp.int32), jax.random.randint(jax.random.fold_in(jax.random.fold_in(_rk, 2), 19), (4096,), 1, 49996, jnp.int32), jax.random.randint(jax.random.fold_in(jax.random.fold_in(_rk, 2), 20), (4096,), 0, 6250, jnp.int32), jax.random.randint(jax.random.fold_in(jax.random.fold_in(_rk, 2), 21), (4096,), 2, 49998, jnp.int32), jax.random.randint(jax.random.fold_in(jax.random.fold_in(_rk, 2), 22), (4096,), 0, 6250, jnp.int32), jax.random.randint(jax.random.fold_in(jax.random.fold_in(_rk, 2), 23), (4096,), 0, 6250, jnp.int32), jax.random.randint(jax.random.fold_in(jax.random.fold_in(_rk, 2), 24), (4096,), 2, 6250, jnp.int32), jax.random.randint(jax.random.fold_in(jax.random.fold_in(_rk, 2), 25), (4096,), 0, 49999, jnp.int32)], axis=0)
        return (r_lS_o, r_lS_i)
    r_lS_o, r_lS_i = _rec_inputs()

    def _L0_rec_setup():
        import jax, jax.numpy as jnp
        import numpy as np
        B = 4096
        D_DENSE = 13
        M = 128
        NTAB = 26
        NROWS = 6250
        BOT = [13, 512, 256, 128]
        TOP = [479, 1024, 1024, 512, 256, 1]
        _NF = NTAB + 1
        _LI, _LJ = np.tril_indices(_NF, k=-1)

        def _mlp(x, ws, bs, sigmoid_layer):
            for i, (w, b) in enumerate(zip(ws, bs)):
                x = x @ w.T + b
                x = jax.nn.sigmoid(x) if i == sigmoid_layer else jax.nn.relu(x)
            return x

        def _apply_emb(emb_w, lS_i, lS_o):
            L = lS_i.shape[1]

            def one(w, idx, off):
                g = w[idx]
                seg = jnp.searchsorted(off, jnp.arange(L), side='right') - 1
                return jax.ops.segment_sum(g, seg, num_segments=B)
            return jax.vmap(one)(emb_w, lS_i, lS_o)
        key = jax.random.key(seed)
        ks = jax.random.split(key, 32)
        inp = {}
        inp['dense_x'] = jax.random.normal(ks[0], (B, D_DENSE), jnp.float32)
        inp['lS_i'] = jax.random.randint(ks[1], (NTAB, B), 0, NROWS)
        inp['lS_o'] = jnp.tile(jnp.arange(B, dtype=jnp.int32), (NTAB, 1))
        inp['emb_w'] = jax.random.normal(ks[2], (NTAB, NROWS, M), jnp.float32) * 0.01
        ki = 3
        for tag, dims in (('bot', BOT), ('top', TOP)):
            for i in range(len(dims) - 1):
                n, m = (dims[i], dims[i + 1])
                std = (2.0 / (n + m)) ** 0.5
                inp[f'{tag}_w{i}'] = jax.random.normal(ks[ki], (m, n), jnp.float32) * std
                inp[f'{tag}_b{i}'] = jax.random.normal(ks[ki + 1], (m,), jnp.float32) * std
                ki += 2
        return inp
    _L0_rec_all = _L0_rec_setup()
    _L0_rec_in = {k: v for k, v in _L0_rec_all.items() if k in ('dense_x', 'emb_w', 'bot_w0', 'bot_b0', 'bot_w1', 'bot_b1', 'bot_w2', 'bot_b2', 'top_w0', 'top_b0', 'top_w1', 'top_b1', 'top_w2', 'top_b2', 'top_w3', 'top_b3', 'top_w4', 'top_b4')}
    del _L0_rec_all
    return {'r_lS_o': r_lS_o, 'r_lS_i': r_lS_i, 'L0_rec_dense_x': _L0_rec_in['dense_x'], 'L0_rec_emb_w': _L0_rec_in['emb_w'], 'L0_rec_bot_w0': _L0_rec_in['bot_w0'], 'L0_rec_bot_b0': _L0_rec_in['bot_b0'], 'L0_rec_bot_w1': _L0_rec_in['bot_w1'], 'L0_rec_bot_b1': _L0_rec_in['bot_b1'], 'L0_rec_bot_w2': _L0_rec_in['bot_w2'], 'L0_rec_bot_b2': _L0_rec_in['bot_b2'], 'L0_rec_top_w0': _L0_rec_in['top_w0'], 'L0_rec_top_b0': _L0_rec_in['top_b0'], 'L0_rec_top_w1': _L0_rec_in['top_w1'], 'L0_rec_top_b1': _L0_rec_in['top_b1'], 'L0_rec_top_w2': _L0_rec_in['top_w2'], 'L0_rec_top_b2': _L0_rec_in['top_b2'], 'L0_rec_top_w3': _L0_rec_in['top_w3'], 'L0_rec_top_b3': _L0_rec_in['top_b3'], 'L0_rec_top_w4': _L0_rec_in['top_w4'], 'L0_rec_top_b4': _L0_rec_in['top_b4']}

def reference(r_lS_o, r_lS_i, L0_rec_dense_x, L0_rec_emb_w, L0_rec_bot_w0, L0_rec_bot_b0, L0_rec_bot_w1, L0_rec_bot_b1, L0_rec_bot_w2, L0_rec_bot_b2, L0_rec_top_w0, L0_rec_top_b0, L0_rec_top_w1, L0_rec_top_b1, L0_rec_top_w2, L0_rec_top_b2, L0_rec_top_w3, L0_rec_top_b3, L0_rec_top_w4, L0_rec_top_b4):
    import jax
    import jax.numpy as jnp

    def _L0_rec_ref(dense_x, lS_o, lS_i, emb_w, bot_w0, bot_b0, bot_w1, bot_b1, bot_w2, bot_b2, top_w0, top_b0, top_w1, top_b1, top_w2, top_b2, top_w3, top_b3, top_w4, top_b4):
        import jax, jax.numpy as jnp
        import numpy as np
        B = 4096
        D_DENSE = 13
        M = 128
        NTAB = 26
        NROWS = 6250
        BOT = [13, 512, 256, 128]
        TOP = [479, 1024, 1024, 512, 256, 1]
        _NF = NTAB + 1
        _LI, _LJ = np.tril_indices(_NF, k=-1)

        def _mlp(x, ws, bs, sigmoid_layer):
            for i, (w, b) in enumerate(zip(ws, bs)):
                x = x @ w.T + b
                x = jax.nn.sigmoid(x) if i == sigmoid_layer else jax.nn.relu(x)
            return x

        def _apply_emb(emb_w, lS_i, lS_o):
            L = lS_i.shape[1]

            def one(w, idx, off):
                g = w[idx]
                seg = jnp.searchsorted(off, jnp.arange(L), side='right') - 1
                return jax.ops.segment_sum(g, seg, num_segments=B)
            return jax.vmap(one)(emb_w, lS_i, lS_o)
        x = _mlp(dense_x, [bot_w0, bot_w1, bot_w2], [bot_b0, bot_b1, bot_b2], -1)
        ly = _apply_emb(emb_w, lS_i, lS_o)
        T = jnp.concatenate([x[:, None, :], jnp.transpose(ly, (1, 0, 2))], axis=1)
        Z = jnp.einsum('bnd,bmd->bnm', T, T)
        Zflat = Z[:, _LI, _LJ]
        R = jnp.concatenate([x, Zflat], axis=1)
        p = _mlp(R, [top_w0, top_w1, top_w2, top_w3, top_w4], [top_b0, top_b1, top_b2, top_b3, top_b4], 4)
        return p
    y = _L0_rec_ref(L0_rec_dense_x, r_lS_o, r_lS_i, L0_rec_emb_w, L0_rec_bot_w0, L0_rec_bot_b0, L0_rec_bot_w1, L0_rec_bot_b1, L0_rec_bot_w2, L0_rec_bot_b2, L0_rec_top_w0, L0_rec_top_b0, L0_rec_top_w1, L0_rec_top_b1, L0_rec_top_w2, L0_rec_top_b2, L0_rec_top_w3, L0_rec_top_b3, L0_rec_top_w4, L0_rec_top_b4)
    return y

_drawn_inputs = setup_inputs


def setup_inputs(seed=0):
    import zlib

    import numpy as np

    out = dict(_drawn_inputs(seed))
    spreads = {}
    factors = {'L0_rec_dense_x': 8.0,
     'L0_rec_emb_w': 8.0,
     'L0_rec_bot_w0': 8.0,
     'L0_rec_bot_b0': 8.0,
     'L0_rec_bot_w1': 8.0,
     'L0_rec_bot_b1': 8.0,
     'L0_rec_bot_w2': 8.0,
     'L0_rec_bot_b2': 23.689,
     'L0_rec_top_b0': 8.0,
     'L0_rec_top_w1': 3.658,
     'L0_rec_top_b1': 54.02,
     'L0_rec_top_w2': 4.15,
     'L0_rec_top_b2': 64.0,
     'L0_rec_top_b3': 23.128}
    for name, (base, spread) in spreads.items():
        noise = np.random.default_rng([zlib.crc32(name.encode()), seed]).standard_normal(out[name].shape)
        drawn = base * np.exp(spread * noise) if base else spread * noise
        out[name] = jnp.asarray(drawn.astype(out[name].dtype))
    for name, factor in factors.items():
        out[name] = (out[name] * factor).astype(out[name].dtype)
    return out
```

```python
import concourse.bass as bass
from concourse import mybir
from contextlib import ExitStack

import numpy as np

P = 128
TABLES = 26
BATCH = 4096
ROWS = 6250
D = 128
J = BATCH // P
TILES = BATCH // P
NF = TABLES + 1
SHIFTS = NF // 2
PAIRS = NF * SHIFTS
NONE = 1 << 20
TREE = BATCH.bit_length() - 1
DENSE = 13
BOT = [512, 256, 128]
TOP = [1024, 1024, 512, 256]
HALF = 12, 14
MB = 512
NB = 256
GROUPS = BATCH // NB
CHUNK = 1024
CHUNKS = 13
JQ = 8
QUARTERS = 4


class Chain:

    def __init__(self, engine, sem):
        self.engine, self.sem, self.base, self.n = engine, sem, 0, 0

    def round(self, r, per_round, before):
        self.base, self.n = r * per_round + before, 0

    def did(self, ins):
        self.n += 1
        ins.then_inc(self.sem, 1)

    def settle(self):
        self.engine.wait_ge(self.sem, self.base + self.n)

    def step(self, ins):
        self.did(ins)
        self.settle()


def view(t, offset, dims, partitions=P, start=0):
    whole = t[:]
    width = whole.ap[0][0]
    return bass.AP(whole.tensor, whole.offset + start * width + offset,
                   [[width, partitions]] + [list(d) for d in dims])


def rec_kernel(nc, offsets, indices, dense_t, emb, bw0, bw1, bw2, bbias, tw0, tws, tw4, tbias, tb4, out):
    f32 = mybir.dt.float32
    f32r = mybir.dt.float32r
    bf16 = mybir.dt.bfloat16
    i32 = mybir.dt.int32
    ALU = mybir.AluOpType
    ACT = mybir.ActivationFunctionType
    AX = mybir.AxisListType

    sums = nc.dram_tensor("sums", [TABLES * BATCH, D], f32).ap()
    last_row = nc.dram_tensor("last_row", [TILES, P, TABLES], i32).ap()
    dense_out = nc.dram_tensor("dense_out", [P, BATCH], f32).ap()
    sums_v = sums.rearrange("(t p j) d -> t p (j d)", p=P, j=J)

    ctx = ExitStack()
    with ctx:
        def sb(name, shape, dt, c=ctx):
            return c.enter_context(nc.sbuf_tensor(name, shape, dt))

        def pb(name, shape, dt, c=ctx):
            return c.enter_context(nc.psum_tensor(name, shape, dt))

        def sem(name):
            return ctx.enter_context(nc.semaphore(name))

        ident = sb("ident", [P, P], f32)
        bias_sb = sb("bias_sb", [P, 22], f32)
        w4_sb = sb("w4_sb", [P, 2], f32)
        b4_sb = sb("b4_sb", [1, 1], f32)
        w0_sb = sb("w0_sb", [P, 4, TOP[0]], f32)
        with ExitStack() as tree:
            off_i = sb("off_i", [TABLES, BATCH], i32, tree)
            first = sb("first", [TABLES, BATCH], f32, tree)
            end = sb("end", [TABLES, BATCH], f32, tree)
            table_base = sb("table_base", [P, TABLES, J], f32, tree)
            idx_work = sb("idx_work", [P, TABLES, J], f32, tree)
        w_hi = sb("w_hi", [P, CHUNKS, 1024], f32r)
        w_lo = sb("w_lo", [P, CHUNKS, 1024], f32r)

        with ExitStack() as one:
            rows = [sb(f"rows{u}", [P, J, D], f32, one) for u in range(2)]
            idx_now = [sb(f"idx_now{u}", [P, J], i32, one) for u in range(2)]
            idx_raw = sb("idx_raw", [P, TABLES + 2, J], i32, one)
            start_hi = sb("start_hi", [P, TABLES + 1, TILES], i32, one)
            start_lo = sb("start_lo", [P, TABLES + 1, TILES], i32, one)
            last_i = sb("last_i", [P, TILES, TABLES], i32, one)
            last_base = sb("last_base", [P, TABLES], f32, one)
            column = sb("column", [P, P], f32, one)
            before = sb("before", [P, P], bf16, one)
            upto = sb("upto", [P, P], bf16, one)
            hot_p = sb("hot_p", [P, TILES, P], bf16, one)
            hot_j = sb("hot_j", [P, TILES, J], bf16, one)
            same = sb("same", [P, J], f32, one)
            begun = sb("begun", [P, J], f32, one)
            starts = sb("starts", [P, 1], f32, one)
            starts_b = sb("starts_b", [P, P], bf16, one)
            runs_upto = sb("runs_upto", [P, 1], f32, one)
            link_m = sb("link_m", [P, P], f32, one)
            xd = sb("xd", [DENSE, MB], f32, one)
            bw0_sb = sb("bw0_sb", [DENSE, BOT[0]], f32, one)
            bw1_sb = sb("bw1_sb", [P, 4, BOT[1]], f32, one)
            bw2_sb = sb("bw2_sb", [P, 2, BOT[2]], f32, one)
            bbias_sb = sb("bbias_sb", [P, 7], f32, one)
            hb0 = sb("hb0", [P, 4, MB], f32, one)
            hb1 = sb("hb1", [P, 2, MB], f32, one)
            xo = sb("xo", [P, MB], f32, one)
            w_raw = sb("w_raw", [P, 1024], f32, one)
            p_tr = [pb(f"p_tr{u}", [P, 16, TABLES], f32, one) for u in range(2)]
            p_start = pb("p_start", [P, J], f32, one)
            p_runs = pb("p_runs", [P, P + 1], f32, one)
            p_carry = pb("p_carry", [P, D], f32, one)
            p_mlp = pb("p_mlp", [P, 2, MB], f32, one)

            s_off, s_idx, s_bw, s_w0 = sem("s_off"), sem("s_idx"), sem("s_bw"), sem("s_w0")
            s_ident, s_masks = sem("s_ident"), sem("s_masks")
            s_pool, s_idxw = sem("s_pool"), sem("s_idxw")
            s_chain = sem("s_chain")
            s_idxnow = [sem(f"s_idxnow{u}") for u in range(2)]
            s_rows = [[sem(f"s_rows{u}{c}") for c in range(QUARTERS)] for u in range(2)]
            s_summed = [sem(f"s_summed{u}") for u in range(2)]
            s_stored = [[sem(f"s_stored{u}{c}") for c in range(QUARTERS)] for u in range(2)]
            s_tree, s_trp, s_trc = sem("s_tree"), sem("s_trp"), sem("s_trc")
            s_lasto = sem("s_lasto")
            s_hot, s_hist, s_starts, s_runs, s_link, s_carry = (
                sem("s_hot"), sem("s_hist"), sem("s_starts"), sem("s_runs"), sem("s_link"), sem("s_carry"))
            s_scan, s_filling = sem("s_scan"), sem("s_filling")
            s_xd, s_mm, s_ev, s_xo = sem("s_xd"), sem("s_mm"), sem("s_ev"), sem("s_xo")
            s_wraw, s_whi, s_wlo = sem("s_wraw"), sem("s_whi"), sem("s_wlo")

            block = one.enter_context(nc.Block())

            @block.sync
            def _(sp):
                sp.dma_start(idx_raw[:, 0:TABLES, :], indices.rearrange("t (p j) -> p t j", j=J)).then_inc(s_idx, 16)
                sp.dma_start(off_i[:], offsets).then_inc(s_off, 16)
                sp.dma_start(bw0_sb[:], bw0).then_inc(s_bw, 16)
                sp.dma_start(bw1_sb[:], bw1.rearrange("(k p) o -> p k o", p=P)).then_inc(s_bw, 16)
                sp.dma_start(bw2_sb[:], bw2.rearrange("(k p) o -> p k o", p=P)).then_inc(s_bw, 16)
                sp.dma_start(bbias_sb[:], bbias).then_inc(s_bw, 16)
                sp.dma_start(bias_sb[:], tbias).then_inc(s_w0, 16)
                sp.dma_start(w4_sb[:], tw4).then_inc(s_w0, 16)
                sp.dma_start(b4_sb[:], tb4).then_inc(s_w0, 16)
                sp.dma_start(w0_sb[:, 0:3, :], tw0[0:3 * P, :].rearrange("(k p) o -> p k o", p=P)).then_inc(s_w0, 16)
                sp.dma_start(w0_sb[0:PAIRS - 2 * P, 3, :], tw0[3 * P:P + PAIRS, :]).then_inc(s_w0, 16)
                sp.wait_ge(s_trc, 4)
                sp.dma_start(last_row.rearrange("i p t -> p i t"), last_i[:]).then_inc(s_lasto, 16)

                def stores(r, u):
                    for c in range(QUARTERS):
                        sp.wait_ge(s_summed[u], r * QUARTERS + c + 1)
                        sp.dma_start(sums_v[bass.ds(r * 2 + u, 1), :, bass.ts(c, JQ * D)].rearrange("a p n -> p (a n)"),
                                     rows[u][:, bass.ts(c, JQ), :].rearrange("p j d -> p (j d)")).then_inc(s_stored[u][c], 16)

                def pair(r, mlp):
                    if not isinstance(r, int):
                        sp.wait_ge(s_whi, r)
                        sp.wait_ge(s_wlo, r)
                    sp.dma_start(w_raw[:], tws[bass.ds(r * P, P), :]).then_inc(s_wraw, 16)
                    if mlp:
                        if not isinstance(r, int):
                            sp.wait_ge(s_mm, r * 7)
                        sp.dma_start(xd[:], dense_t[:, bass.ds(r * MB, MB)]).then_inc(s_xd, 16)
                    stores(r, 0)
                    if mlp:
                        sp.wait_ge(s_ev, r * 7 + 7)
                        sp.dma_start(dense_out[:, bass.ds(r * MB, MB)], xo[:]).then_inc(s_xo, 16)
                    stores(r, 1)

                pair(0, True)
                with sp.Fori(1, BATCH // MB) as r:
                    pair(r, True)
                with sp.Fori(BATCH // MB, TABLES // 2) as r:
                    pair(r, False)
                sp.wait_ge(s_xo, 16 * (BATCH // MB))
                sp.wait_ge(s_lasto, 16)
                sp.wait_ge(s_w0, 80)
                for u in range(2):
                    for c in range(QUARTERS):
                        sp.wait_ge(s_stored[u][c], 16 * (TABLES // 2))

            @block.gpsimd
            def _(pool):
                pool.iota(table_base[:], pattern=[[ROWS, TABLES], [0, J]], base=0, channel_multiplier=0,
                          allow_small_or_imprecise_dtypes=True).then_inc(s_pool, 1)
                pool.iota(last_base[:], pattern=[[BATCH, TABLES]], base=-1, channel_multiplier=0,
                          allow_small_or_imprecise_dtypes=True).then_inc(s_pool, 1)
                pool.iota(column[:], pattern=[[1, P]], base=0, channel_multiplier=0,
                          allow_small_or_imprecise_dtypes=True).then_inc(s_pool, 1)
                pool.memset(ident[:], 0.0).then_inc(s_ident, 1)
                pool.memset(before[:], 1.0).then_inc(s_ident, 1)
                pool.memset(upto[:], 1.0).then_inc(s_ident, 1)
                pool.wait_ge(s_ident, 3)
                pool.affine_select(out=ident[:], in_=ident[:], compare_op=ALU.not_equal, fill=1.0,
                                   base=0, pattern=[[-1, P]], channel_multiplier=1).then_inc(s_masks, 1)
                pool.affine_select(out=before[:], in_=before[:], compare_op=ALU.is_gt, fill=0.0,
                                   base=0, pattern=[[1, P]], channel_multiplier=-1).then_inc(s_masks, 1)
                pool.affine_select(out=upto[:], in_=upto[:], compare_op=ALU.is_ge, fill=0.0,
                                   base=0, pattern=[[1, P]], channel_multiplier=-1).then_inc(s_masks, 1)

                def gather(r, u):
                    pool.wait_ge(s_idxnow[u], r + 1)
                    for j in range(J):
                        if j % JQ == 0 and not isinstance(r, int):
                            pool.wait_ge(s_stored[u][j // JQ], r * 16)
                            pool.sem_inc(s_filling, 1)
                        pool.indirect_dma_start(
                            out=rows[u][:, j, :], out_offset=None, in_=emb,
                            in_offset=bass.IndirectOffsetOnAxis(ap=idx_now[u][:, j:j + 1], axis=0)).then_inc(s_rows[u][j // JQ], 16)

                gather(0, 0)
                gather(0, 1)
                with pool.Fori(1, TABLES // 2) as r:
                    gather(r, 0)
                    gather(r, 1)

            @block.scalar
            def _(act):
                def dense_step(r):
                    if isinstance(r, int):
                        act.wait_ge(s_bw, 64)
                    else:
                        act.wait_ge(s_xo, r * 16)
                    for n in range(7):
                        dst = hb0[:, n, :] if n < 4 else hb1[:, n - 4, :] if n < 6 else xo[:]
                        act.wait_ge(s_mm, r * 7 + n + 1)
                        nc.scalar.activation(dst, p_mlp[:, n % 2, :], ACT.Relu,
                                             bias=bbias_sb[:, n:n + 1]).then_inc(s_ev, 1)

                def split_hi(r):
                    act.wait_ge(s_wraw, r * 16 + 16)
                    nc.scalar.activation(w_hi[:, bass.ds(r, 1), :].rearrange("p a n -> p (a n)"), w_raw[:],
                                         ACT.Copy).then_inc(s_whi, 1)

                dense_step(0)
                split_hi(0)
                with act.Fori(1, BATCH // MB) as r:
                    dense_step(r)
                    split_hi(r)
                with act.Fori(BATCH // MB, TABLES // 2) as r:
                    split_hi(r)

            @block.vector
            def _(dve):
                chain = Chain(dve, s_chain)

                raw = idx_raw[:, 0:TABLES, :]
                chain.did(nc.vector.memset(idx_raw[:, TABLES:TABLES + 2, :], 0))
                chain.did(nc.vector.memset(start_hi[:, TABLES:TABLES + 1, :], 0))
                chain.did(nc.vector.memset(start_lo[:, TABLES:TABLES + 1, :], 0))
                dve.wait_ge(s_idx, 16)
                dve.wait_ge(s_pool, 3)
                chain.step(nc.vector.tensor_scalar(idx_work[:], raw, 0.0, float(ROWS), ALU.is_lt, ALU.mult))
                chain.step(nc.vector.tensor_tensor(idx_work[:], idx_work[:], raw, ALU.add))
                chain.step(nc.vector.tensor_scalar(idx_work[:], idx_work[:], 0.0, float(ROWS - 1), ALU.max, ALU.min))
                chain.step(nc.vector.tensor_tensor(raw, idx_work[:], table_base[:], ALU.add))
                for u in range(2):
                    nc.vector.tensor_copy(idx_now[u][:], idx_raw[:, u, :]).then_inc(s_idxnow[u], 1)

                chain.did(nc.vector.memset(first[:, 0:1], 0.0))
                chain.did(nc.vector.memset(end[:, 0:1], float(BATCH)))
                dve.wait_ge(s_off, 16)
                chain.settle()

                def every(t, start, step):
                    return t[:, start:BATCH:step]

                for level in range(TREE):
                    width = BATCH >> level
                    half = width // 2
                    chain.did(nc.vector.tensor_tensor(every(first, half, width), every(first, 0, width),
                                                      every(off_i, half, width), ALU.max))
                    chain.step(nc.vector.tensor_copy(every(end, half, width), every(end, 0, width)))
                    chain.step(nc.vector.tensor_tensor(every(end, 0, width), every(end, 0, width),
                                                       every(off_i, half, width), ALU.min))
                chain.step(nc.vector.tensor_tensor(first[:, 0:1], first[:, 0:1], off_i[:, 0:1], ALU.max))
                holds = off_i[:].bitcast(f32)
                chain.step(nc.vector.tensor_tensor(holds, end[:], first[:], ALU.is_gt))
                chain.did(nc.vector.scalar_tensor_tensor(first[:], first[:], float(-NONE), holds, ALU.add, ALU.mult))
                chain.step(nc.vector.scalar_tensor_tensor(end[:], end[:], float(-NONE), holds, ALU.add, ALU.mult))
                nc.vector.tensor_scalar(first[:], first[:], float(NONE), None, ALU.add).then_inc(s_tree, 1)
                nc.vector.tensor_scalar(end[:], end[:], float(NONE), None, ALU.add).then_inc(s_tree, 1)

                for n in range(4):
                    lo = 16 * (n // 2)
                    dve.wait_ge(s_trp, n + 1)
                    if n % 2 == 0:
                        nc.vector.tensor_copy(start_lo[:, 0:TABLES, lo:lo + 16].rearrange("p t i -> p i t"),
                                              p_tr[0][:]).then_inc(s_trc, 1)
                    else:
                        nc.vector.tensor_tensor(last_i[:, lo:lo + 16, :], p_tr[1][:],
                                                last_base[:].unsqueeze(1).to_broadcast([P, 16, TABLES]),
                                                ALU.add).then_inc(s_trc, 1)
                dve.wait_ge(s_trc, 4)
                chain.step(nc.vector.tensor_scalar(start_hi[:, 0:TABLES, :], start_lo[:, 0:TABLES, :],
                                                   J.bit_length() - 1, None, ALU.arith_shift_right))
                chain.step(nc.vector.tensor_scalar(start_lo[:, 0:TABLES, :], start_lo[:, 0:TABLES, :],
                                                   J - 1, None, ALU.bitwise_and))

                def hot(t):
                    hi = start_hi[:, bass.ds(t, 1), :].rearrange("p a n -> p (a n)")
                    lo = start_lo[:, bass.ds(t, 1), :].rearrange("p a n -> p (a n)")
                    nc.vector.tensor_tensor(hot_p[:], hi.unsqueeze(2).to_broadcast([P, TILES, P]),
                                            column[:].unsqueeze(1).to_broadcast([P, TILES, P]),
                                            ALU.is_equal).then_inc(s_hot, 1)
                    nc.vector.tensor_tensor(hot_j[:], lo.unsqueeze(2).to_broadcast([P, TILES, J]),
                                            column[:, 0:J].unsqueeze(1).to_broadcast([P, TILES, J]),
                                            ALU.is_equal).then_inc(s_hot, 1)

                def runs(t):
                    dve.wait_ge(s_hist, t + 1)
                    chain.did(nc.vector.tensor_scalar(same[:], p_start[:], -1.0, 1.0, ALU.mult, ALU.add))
                    chain.step(nc.vector.reduce_sum(starts[:], p_start[:], AX.X))
                    nc.vector.tensor_copy(starts_b[:], starts[:].to_broadcast([P, P])).then_inc(s_starts, 1)
                    chain.did(nc.vector.tensor_tensor_scan(begun[:], same[:], same[:], 1.0, ALU.mult, ALU.mult))
                    dve.wait_ge(s_runs, t + 1)
                    chain.step(nc.vector.tensor_copy(runs_upto[:], p_runs[:, P:P + 1]))
                    nc.vector.scalar_tensor_tensor(link_m[:], p_runs[:, 0:P], runs_upto[:], before[:],
                                                   ALU.is_equal, ALU.mult).then_inc(s_link, 1)

                def table(r, u):
                    t = r * 2 + u
                    for j in range(1, J):
                        if j == 1 or j % JQ == 0:
                            dve.wait_ge(s_rows[u][j // JQ], (r + 1) * (16 * JQ))
                        if j == J - JQ:
                            nc.vector.tensor_copy(idx_now[u][:],
                                                  idx_raw[:, bass.ds(t + 2, 1), :].rearrange("p a j -> p (a j)")
                                                  ).then_inc(s_idxnow[u], 1)
                        ins = nc.vector.scalar_tensor_tensor(rows[u][:, j, :], rows[u][:, j - 1, :], same[:, j:j + 1],
                                                             rows[u][:, j, :], ALU.mult, ALU.add)
                        if j < J - 1:
                            chain.step(ins)
                    ins.then_inc(s_scan, 1)
                    dve.wait_ge(s_carry, t + 1)
                    for j in range(J):
                        ins = nc.vector.scalar_tensor_tensor(rows[u][:, j, :], p_carry[:], begun[:, j:j + 1],
                                                             rows[u][:, j, :], ALU.mult, ALU.add)
                        if j % JQ == JQ - 1:
                            ins.then_inc(s_summed[u], 1)
                    hot(t + 1)
                    dve.wait_ge(s_summed[u], (r + 1) * QUARTERS)
                    runs(t + 1)

                def split_lo(r):
                    dve.wait_ge(s_whi, r + 1)
                    nc.vector.tensor_tensor(w_lo[:, bass.ds(r, 1), :].rearrange("p a n -> p (a n)"), w_raw[:],
                                            w_hi[:, bass.ds(r, 1), :].rearrange("p a n -> p (a n)").bitcast(f32),
                                            ALU.subtract).then_inc(s_wlo, 1)

                hot(0)
                runs(0)
                ahead = chain.n
                per_round = 2 * (J - 2 + 4)
                chain.n = 0
                with dve.Fori(0, TABLES // 2) as r:
                    chain.round(r, per_round, ahead)
                    table(r, 0)
                    table(r, 1)
                    split_lo(r)
                    assert chain.n == per_round

            @block.tensor
            def _(pe):
                pe.wait_ge(s_tree, 2)
                pe.wait_ge(s_masks, 3)
                for n in range(4):
                    if n >= 2:
                        pe.wait_ge(s_trc, n - 1)
                    src = first if n % 2 == 0 else end
                    for m in range(16):
                        i = 16 * (n // 2) + m
                        ins = nc.tensor.transpose(p_tr[n % 2][:, m, :], src[:, bass.ts(i, P)],
                                                  ident[0:TABLES, 0:TABLES])
                    ins.then_inc(s_trp, 1)

                def runs(t):
                    pe.wait_ge(s_hot, (t + 1) * 2)
                    for i in range(TILES):
                        ins = nc.tensor.matmul(p_start[:], hot_p[:, i, :], hot_j[:, i, :],
                                               start=(i == 0), stop=(i == TILES - 1))
                    ins.then_inc(s_hist, 1)
                    pe.wait_ge(s_starts, t + 1)
                    nc.tensor.matmul(p_runs[:, 0:P], starts_b[:], before[:], start=True, stop=True)
                    nc.tensor.matmul(p_runs[:, P:P + 1], upto[:], starts_b[:, 0:1], start=True, stop=True
                                     ).then_inc(s_runs, 1)

                def carry(t, u):
                    pe.wait_ge(s_link, t + 1)
                    pe.wait_ge(s_scan, t + 1)
                    nc.tensor.matmul(p_carry[:], link_m[:], rows[u][:, J - 1, :], start=True, stop=True
                                     ).then_inc(s_carry, 1)

                def dense_step(r):
                    pe.wait_ge(s_xd, r * 16 + 16)
                    for n in range(7):
                        bank = p_mlp[:, n % 2, :]
                        at = {4: 4, 5: 4, 6: 6}.get(n, n - 1)
                        if not isinstance(r, int) or at > 0:
                            pe.wait_ge(s_ev, r * 7 + at)
                        if n < 4:
                            ins = nc.tensor.matmul(bank, bw0_sb[:, bass.ts(n, P)], xd[:], start=True, stop=True)
                        elif n < 6:
                            for k in range(4):
                                ins = nc.tensor.matmul(bank, bw1_sb[:, k, bass.ts(n - 4, P)], hb0[:, k, :],
                                                       start=(k == 0), stop=(k == 3))
                        else:
                            for k in range(2):
                                ins = nc.tensor.matmul(bank, bw2_sb[:, k, :], hb1[:, k, :],
                                                       start=(k == 0), stop=(k == 1))
                        ins.then_inc(s_mm, 1)

                runs(0)
                pe.wait_ge(s_bw, 64)
                carry(0, 0)
                dense_step(0)
                runs(1)
                carry(1, 1)
                runs(2)
                with pe.Fori(1, BATCH // MB) as r:
                    carry(r * 2, 0)
                    dense_step(r)
                    runs(r * 2 + 1)
                    carry(r * 2 + 1, 1)
                    runs(r * 2 + 2)
                with pe.Fori(BATCH // MB, TABLES // 2) as r:
                    carry(r * 2, 0)
                    runs(r * 2 + 1)
                    carry(r * 2 + 1, 1)
                    runs(r * 2 + 2)

        with ExitStack() as two:
            bags = [sb(f"bags{b}", [P, HALF[b], D], f32, two) for b in range(2)]
            feat_t = sb("feat_t", [P, P, 32], f32, two)
            dots = sb("dots", [P, NF, 32], f32, two)
            dots_t = sb("dots_t", [P, NF + SHIFTS, 32], f32, two)
            pairs = sb("pairs", [P, PAIRS], f32, two)
            top_in = sb("top_in", [P, 4, NB], f32, two)
            act_a = [sb(f"act_a_{part}", [P, 8, NB], f32r, two) for part in ("hi", "lo")]
            act_b = [sb(f"act_b_{part}", [P, 8, NB], f32r, two) for part in ("hi", "lo")]
            act_3 = sb("act_3", [P, 2, NB], f32, two)
            whole = [sb(f"whole{u}", [P, NB], f32, two) for u in range(2)]
            fetch_row = [sb(f"fetch_row{a}", [P, TABLES], i32, two) for a in range(2)]
            dense_in = sb("dense_in", [P, NB], f32, two)
            prob = sb("prob", [1, NB], f32, two)
            p_t = pb("p_t", [P, 2, 4, P], f32, two)
            p_z = pb("p_z", [P, 2, 512], f32, two)
            p_r = pb("p_r", [P, 4, P], f32, two)
            p_m = pb("p_m", [P, 3, 512], f32, two)

            s_row = [sem(f"s_row{a}") for a in range(2)]
            s_fetch2 = sem("s_fetch2")
            s_bags = [sem(f"s_bags{b}") for b in range(2)]
            s_zero = [sem(f"s_zero{b}") for b in range(2)]
            s_dense, s_topx, s_featx, s_pad = sem("s_dense"), sem("s_topx"), sem("s_featx"), sem("s_pad")
            s_t, s_tfree = sem("s_t"), sem("s_tfree")
            s_z, s_zact, s_zdve, s_zt, s_dt, s_pairs = (
                sem("s_z"), sem("s_zact"), sem("s_zdve"), sem("s_zt"), sem("s_dt"), sem("s_pairs"))
            s_r, s_rfree = sem("s_r"), sem("s_rfree")
            s_m, s_mfree, s_hi, s_lo = sem("s_m"), sem("s_mfree"), sem("s_hi"), sem("s_lo")
            s_out = sem("s_out")

            NT, NZ = (TABLES + 3) // 4, P // 16
            K_TILES = (4, 8, 8, 4, 2)
            PARTS = (2, 2, 2, 1, 1)
            M_BEFORE = (0, 8, 16, 20, 22)
            NM = 23
            mlp = [("M", layer, (o, part)) for layer, tiles in enumerate((8, 8, 4, 2, 1))
                   for o in range(tiles) for part in range(PARTS[layer])]
            ahead = {}
            for a, slots in enumerate(((0, 1, 2, 9, 10, 11, 12), (22, 23, 24, 29, 30, 31, 32))):
                for c, slot in enumerate(slots):
                    ahead.setdefault(slot, []).append(("T", a, c))
            for a, slots in enumerate(((13, 15, 16, 17, 18, 19, 20, 21), (33, 34, 35, 36, 37, 38, 39, 40))):
                for c, slot in enumerate(slots):
                    ahead.setdefault(slot, []).append(("Z", a, c))
            ahead[24].append(("R", 0, 0))
            ahead[42] = [("R", 1, 0)]
            order = []
            for slot, m in enumerate(mlp):
                order += ahead.get(slot, []) + [m]

            def steps(kind_inter, kind_mlp, handlers, g):
                for kind, x, y in order:
                    if kind == "M" and kind_mlp:
                        handlers[kind](g, x, y)
                    if kind != "M" and kind_inter:
                        handlers[kind](g + 1, x, y)

            def rounds(engine, handlers, round_start=None):
                for g in (-1, 0):
                    if round_start:
                        round_start(g, True)
                    steps(True, g >= 0, handlers, g)
                with engine.Fori(1, GROUPS - 1) as g:
                    if round_start:
                        round_start(g, True)
                    steps(True, True, handlers, g)
                if round_start:
                    round_start(GROUPS - 1, False)
                steps(False, True, handlers, GROUPS - 1)

            def wait(engine, semaphore, value):
                if not isinstance(value, int) or value > 0:
                    engine.wait_ge(semaphore, value)

            def tables_of(c):
                return range(4 * c, min(4 * c + 4, TABLES))

            block = two.enter_context(nc.Block())

            @block.sync
            def _(sp):
                def inputs(g):
                    tile = g * 2 if isinstance(g, int) else sp.snap(g * 2)
                    for a in range(2):
                        wait(sp, s_t, (tile + (a - 1)) * NT)
                        sp.dma_start(fetch_row[a][:], last_row[bass.ds(tile + a, 1), :, :].rearrange("a p t -> p (a t)")
                                     ).then_inc(s_row[a], 16)
                        if a == 0:
                            wait(sp, s_featx, g * 2)
                            sp.dma_start(dense_in[:], dense_out[:, bass.ds(g * NB, NB)]).then_inc(s_dense, 16)

                inputs(0)
                inputs(1)
                with sp.Fori(2, GROUPS) as g:
                    inputs(g)

            @block.gpsimd
            def _(pool):
                def fetch(g, a):
                    pool.wait_ge(s_row[a], (g + 1) * 16)
                    for b in range(2):
                        pool.wait_ge(s_zero[b], g * 2 + (a + 1))
                        if not isinstance(g, int):
                            pool.sem_inc(s_fetch2, 1)
                        for n in range(HALF[b]):
                            t = HALF[0] * b + n
                            pool.indirect_dma_start(
                                out=bags[b][:, n, :], out_offset=None, in_=sums,
                                in_offset=bass.IndirectOffsetOnAxis(ap=fetch_row[a][:, t:t + 1], axis=0),
                                bounds_check=TABLES * BATCH - 1, oob_is_err=False).then_inc(s_bags[b], 16)

                fetch(0, 0)
                fetch(0, 1)
                with pool.Fori(1, GROUPS) as g:
                    fetch(g, 0)
                    fetch(g, 1)

            @block.tensor
            def _(pe):
                def transposes(g, a, c):
                    i = g * 2 + a
                    if c in (0, 3):
                        pe.wait_ge(s_bags[c // 3], (i + 1) * (16 * HALF[c // 3]))
                    wait(pe, s_tfree, g * (2 * NT) + a * NT + c - 1)
                    for n, t in enumerate(tables_of(c)):
                        ins = nc.tensor.transpose(p_t[:, (a * NT + c) % 2, n, :], bags[0 if t < HALF[0] else 1][:, t if t < HALF[0] else t - HALF[0], :], ident[:])
                    ins.then_inc(s_t, 1)

                def dot(g, a, c):
                    if c == 0:
                        pe.wait_ge(s_tfree, g * (2 * NT) + (a + 1) * NT)
                        pe.wait_ge(s_featx, g * 2 + a + 1)
                    wait(pe, s_zact, g * (2 * NZ) + a * NZ + c - 1)
                    wait(pe, s_zdve, g * (2 * NZ) + a * NZ + c - 1)
                    for n in range(4):
                        four = feat_t[:, bass.ts(4 * c + n, 4), :]
                        ins = nc.tensor.matmul(p_z[:, c % 2, bass.ts(n, 4 * NF)],
                                               four.rearrange("p i f -> p (i f)"), four[:, :, 0:NF],
                                               start=True, stop=True)
                    ins.then_inc(s_z, 1)

                def pair_transposes(g, a, _):
                    pe.wait_ge(s_pairs, g * 2 + a + 1)
                    wait(pe, s_rfree, g * 2 + a)
                    for n in range(3):
                        width = min(P, PAIRS - n * P)
                        ins = nc.tensor.transpose(p_r[0:width, n, :], pairs[:, n * P:n * P + width], ident[:])
                    ins.then_inc(s_r, 1)

                def product(g, layer, tile_part):
                    o, part = tile_part
                    m = M_BEFORE[layer] + o
                    bank = p_m[0:1 if layer == 4 else P, m % 3, 0:NB]
                    last = m - 3 if m >= 3 else max(x for x in range(NM) if x % 3 == m % 3) - NM
                    if part == 0:
                        wait(pe, s_mfree, g * NM + last + 1)
                    if layer == 0 and o == 0 and part == 0:
                        pe.wait_ge(s_rfree, g * 2 + 2)
                        pe.wait_ge(s_topx, g * 16 + 16)
                    K = K_TILES[layer]
                    for k in range(part * K // PARTS[layer], (part + 1) * K // PARTS[layer]):
                        if o == 0 and layer in (1, 2, 3):
                            pe.wait_ge(s_lo, g * 20 + M_BEFORE[layer - 1] + k + 1)
                        if layer == 4 and k == 0:
                            pe.wait_ge(s_mfree, g * NM + NM - 1)
                        if layer == 0:
                            rows_k = P if k < 3 else PAIRS - 2 * P
                            ins = nc.tensor.matmul(bank, w0_sb[0:rows_k, k, bass.ts(o, P)], top_in[0:rows_k, k, :],
                                                   start=(k == 0), stop=(k == K - 1))
                        elif layer == 4:
                            ins = nc.tensor.matmul(bank, w4_sb[:, k:k + 1], act_3[:, k, :],
                                                   start=(k == 0), stop=(k == K - 1))
                        else:
                            hi, lo = act_b if layer == 2 else act_a
                            if layer == 1:
                                at = (k, o * P)
                            elif layer == 2:
                                at = (8 + k // 2, (k % 2) * TOP[2] + o * P)
                            else:
                                at = (12, k * TOP[3] + o * P)
                            wh = w_hi[:, at[0], at[1]:at[1] + P]
                            wl = w_lo[:, at[0], at[1]:at[1] + P]
                            nc.tensor.matmul(bank, wh, hi[:, k, :], start=(k == 0), stop=False)
                            nc.tensor.matmul(bank, wh, lo[:, k, :], start=False, stop=False)
                            ins = nc.tensor.matmul(bank, wl, hi[:, k, :], start=False, stop=(k == K - 1))
                    if k == K - 1:
                        ins.then_inc(s_m, 1)

                pe.wait_ge(s_pad, 1)
                rounds(pe, {"T": transposes, "Z": dot, "R": pair_transposes, "M": product})

            def drop_dots(engine_copy, g, a, c, side):
                for i in (2 * side, 2 * side + 1):
                    ins = engine_copy(
                        view(dots, 4 * c, [[1, 4], [32, NF]], 32, 32 * i),
                        view(p_z, 512 * (c % 2) + i * NF, [[4 * NF, 4], [1, NF]], 32, 32 * i))
                return ins

            @block.scalar
            def _(act):
                def features(g, a, c):
                    n = len(tables_of(c))
                    act.wait_ge(s_t, g * (2 * NT) + a * NT + c + 1)
                    if c == 0:
                        wait(act, s_z, g * (2 * NZ) + a * NZ)
                    nc.scalar.activation(
                        view(feat_t, 1 + 4 * c, [[1, n], [32, 4], [P, 32]]),
                        p_t[:, (a * NT + c) % 2, 0:n, :].rearrange("p n (i s) -> p n i s", i=4),
                        ACT.Copy).then_inc(s_tfree, 1)

                def dots_out(g, a, c):
                    act.wait_ge(s_z, g * (2 * NZ) + a * NZ + c + 1)
                    if c == 0:
                        wait(act, s_zt, g * 2 + a)
                    drop_dots(lambda o, i: nc.scalar.activation(o, i, ACT.Copy), g, a, c, 0).then_inc(s_zact, 1)

                def top_in_pairs(g, a, _):
                    act.wait_ge(s_r, g * 2 + a + 1)
                    wait(act, s_m, (g - 1) * NM + 8)
                    nc.scalar.activation(top_in[:, 1:3, bass.ts(a, P)], p_r[:, 0:2, :], ACT.Copy)
                    nc.scalar.activation(top_in[0:PAIRS - 2 * P, 3, bass.ts(a, P)], p_r[0:PAIRS - 2 * P, 2, :], ACT.Copy
                                         ).then_inc(s_rfree, 1)

                def dense_features(g):
                    act.dma_start(top_in[:, 0, :], dense_out[:, bass.ds(g * NB, NB)]).then_inc(s_topx, 16)

                def layer_out(g, layer, tile_part):
                    o, part = tile_part
                    if part < PARTS[layer] - 1:
                        return
                    m = M_BEFORE[layer] + o
                    act.wait_ge(s_m, g * NM + m + 1)
                    if m == 7 and not (isinstance(g, int) and g == GROUPS - 1):
                        dense_features(g + 1)
                    if layer == 4:
                        wait(act, s_out, g * 16)
                        nc.scalar.activation(prob[:], p_m[0:1, m % 3, 0:NB], ACT.Sigmoid, bias=b4_sb[:]).then_inc(s_mfree, 1)
                        act.wait_ge(s_mfree, g * NM + NM)
                        act.dma_start(out[bass.ds(g * NB, NB), :].rearrange("b a -> a b"), prob[:]).then_inc(s_out, 16)
                        return
                    bias = bias_sb[:, m:m + 1]
                    bank = p_m[:, m % 3, 0:NB]
                    if layer == 3:
                        nc.scalar.activation(act_3[:, o, :], bank, ACT.Relu, bias=bias).then_inc(s_mfree, 1)
                        return
                    wait(act, s_lo, g * 20 + m - 1)
                    nc.scalar.activation(whole[m % 2][:], bank, ACT.Relu, bias=bias)
                    hi = (act_b if layer == 1 else act_a)[0]
                    nc.scalar.activation(hi[:, o, :], bank, ACT.Relu, bias=bias).then_inc(s_mfree, 1)

                dense_features(0)
                rounds(act, {"T": features, "Z": dots_out, "R": top_in_pairs, "M": layer_out})
                act.wait_ge(s_out, 16 * GROUPS)

            @block.vector
            def _(dve):
                def features(g, a, c):
                    if c == 0:
                        if a == 0:
                            dve.wait_ge(s_dense, g * 16 + 16)
                        wait(dve, s_z, g * (2 * NZ) + a * NZ)
                        nc.vector.tensor_copy(view(feat_t, 0, [[32, 4], [P, 32]]),
                                              dense_in[:, bass.ts(a, P)].rearrange("p (i s) -> p i s", i=4)
                                              ).then_inc(s_featx, 1)
                    if c in (2, NT - 1):
                        b = 0 if c == 2 else 1
                        dve.wait_ge(s_t, g * (2 * NT) + a * NT + c + 1)
                        nc.vector.memset(bags[b][:], 0.0).then_inc(s_zero[b], 1)

                def dots_out(g, a, c):
                    dve.wait_ge(s_z, g * (2 * NZ) + a * NZ + c + 1)
                    if c == 0:
                        wait(dve, s_zt, g * 2 + a)
                    drop_dots(nc.vector.tensor_copy, g, a, c, 1).then_inc(s_zdve, 1)
                    if c == NZ - 1:
                        n = g * 2 + a + 1
                        dve.wait_ge(s_zact, g * (2 * NZ) + (a + 1) * NZ)
                        dve.wait_ge(s_zdve, g * (2 * NZ) + (a + 1) * NZ)
                        nc.vector.transpose(dots_t[:, 0:NF, :].rearrange("p m n -> p (m n)"),
                                            dots[:].rearrange("p m s -> p (m s)")).then_inc(s_zt, 1)
                        dve.wait_ge(s_zt, n)
                        nc.vector.tensor_copy(dots_t[:, NF:NF + SHIFTS, :], dots_t[:, 0:SHIFTS, :]).then_inc(s_dt, 1)
                        dve.wait_ge(s_dt, n)
                        wait(dve, s_r, n - 1)
                        nc.vector.tensor_copy(pairs[:].rearrange("p (k n) -> p k n", n=NF),
                                              view(dots_t, 32, [[32, SHIFTS], [33, NF]])).then_inc(s_pairs, 1)

                def layer_out(g, layer, tile_part):
                    o, part = tile_part
                    if part < PARTS[layer] - 1:
                        return
                    if layer < 3:
                        m = M_BEFORE[layer] + o
                        dve.wait_ge(s_mfree, g * NM + m + 1)
                        hi, lo = act_b if layer == 1 else act_a
                        nc.vector.tensor_tensor(lo[:, o, :], whole[m % 2][:], hi[:, o, :].bitcast(f32),
                                                ALU.subtract).then_inc(s_lo, 1)

                nc.vector.memset(feat_t[:, :, NF:32], 0.0).then_inc(s_pad, 1)
                for b in range(2):
                    nc.vector.memset(bags[b][:], 0.0).then_inc(s_zero[b], 1)
                rounds(dve, {"T": features, "Z": dots_out, "R": lambda g, a, c: None, "M": layer_out})



def kernel(r_lS_o, r_lS_i, L0_rec_dense_x, L0_rec_emb_w,
           L0_rec_bot_w0, L0_rec_bot_b0, L0_rec_bot_w1, L0_rec_bot_b1, L0_rec_bot_w2, L0_rec_bot_b2,
           L0_rec_top_w0, L0_rec_top_b0, L0_rec_top_w1, L0_rec_top_b1, L0_rec_top_w2, L0_rec_top_b2,
           L0_rec_top_w3, L0_rec_top_b3, L0_rec_top_w4, L0_rec_top_b4):
    import concourse.bacc as bacc
    from concourse.bass_utils import run_bass_kernel_spmd

    def cols(*biases):
        return np.concatenate([np.reshape(b, (-1, P)).T for b in biases], axis=1)

    order = list(range(P))
    for k in range(1, SHIFTS + 1):
        for n in range(NF):
            hi, lo = max(n, (n + k) % NF), min(n, (n + k) % NF)
            order.append(P + hi * (hi - 1) // 2 + lo)
    w0, w1, w2, w3 = (np.asarray(w) for w in (L0_rec_top_w0, L0_rec_top_w1, L0_rec_top_w2, L0_rec_top_w3))
    chunks = np.concatenate([
        w1.T,
        w2.T.reshape(4, 2, P, TOP[2]).transpose(0, 2, 1, 3).reshape(4 * P, CHUNK),
        w3.T.reshape(4, P, TOP[3]).transpose(1, 0, 2).reshape(P, CHUNK),
    ])
    arrays = {
        "offsets": np.asarray(r_lS_o),
        "indices": np.asarray(r_lS_i),
        "dense_t": np.asarray(L0_rec_dense_x).T,
        "emb": np.reshape(L0_rec_emb_w, (TABLES * ROWS, D)),
        "bw0": np.asarray(L0_rec_bot_w0).T,
        "bw1": np.asarray(L0_rec_bot_w1).T,
        "bw2": np.asarray(L0_rec_bot_w2).T,
        "bbias": cols(L0_rec_bot_b0, L0_rec_bot_b1, L0_rec_bot_b2),
        "tw0": w0.T[order],
        "tws": chunks,
        "tw4": cols(L0_rec_top_w4),
        "tbias": cols(L0_rec_top_b0, L0_rec_top_b1, L0_rec_top_b2, L0_rec_top_b3),
        "tb4": np.reshape(L0_rec_top_b4, (1, 1)),
    }
    arrays = {name: np.ascontiguousarray(a) for name, a in arrays.items()}
    nc = bacc.Bacc("TRN2", target_bir_lowering=False, num_devices=1)
    args = [nc.dram_tensor(name, a.shape, mybir.dt.from_np(a.dtype), kind="ExternalInput").ap()
            for name, a in arrays.items()]
    out = nc.dram_tensor("out", (BATCH, 1), mybir.dt.float32, kind="ExternalOutput").ap()
    rec_kernel(nc, *args, out)
    r = run_bass_kernel_spmd(nc, [arrays], core_ids=[0])
    return r.results[0]["out"]
```

```python
import concourse.bass as bass
from concourse import mybir
from contextlib import ExitStack

import numpy as np

P = 128
TABLES = 26
BATCH = 4096
ROWS = 6250
D = 128
J = BATCH // P
TILES = BATCH // P
NF = TABLES + 1
SHIFTS = NF // 2
PAIRS = NF * SHIFTS
NONE = 1 << 20
TREE = BATCH.bit_length() - 1
DENSE = 13
BOT = [512, 256, 128]
TOP = [1024, 1024, 512, 256]
HALF = 12, 14
MB = 256
STEPS = BATCH // MB
ND = 15
NB = 256
GROUPS = BATCH // NB
CHUNK = 1024
CHUNKS = STEPS
PAIR_CHUNK = 13
SHORT = PAIRS - 2 * P
JQ = 8
QUARTERS = 4


class Chain:

    def __init__(self, engine, sem):
        self.engine, self.sem, self.base, self.n = engine, sem, 0, 0

    def round(self, r, per_round, before):
        self.base, self.n = r * per_round + before, 0

    def did(self, ins):
        self.n += 1
        ins.then_inc(self.sem, 1)

    def settle(self):
        self.engine.wait_ge(self.sem, self.base + self.n)

    def step(self, ins):
        self.did(ins)
        self.settle()


def view(t, offset, dims, partitions=P, start=0):
    whole = t[:]
    width = whole.ap[0][0]
    return bass.AP(whole.tensor, whole.offset + start * width + offset,
                   [[width, partitions]] + [list(d) for d in dims])


def rec_kernel(nc, offsets, indices, dense_t, emb, bw0, bw1, bw2, bbias, tw0x, tws, tw4, tbias, tb4, out):
    f32 = mybir.dt.float32
    f32r = mybir.dt.float32r
    bf16 = mybir.dt.bfloat16
    i32 = mybir.dt.int32
    ALU = mybir.AluOpType
    ACT = mybir.ActivationFunctionType
    AX = mybir.AxisListType

    sums = nc.dram_tensor("sums", [TABLES * BATCH, D], f32).ap()
    last_row = nc.dram_tensor("last_row", [TILES, P, TABLES], i32).ap()
    dense_out = nc.dram_tensor("dense_out", [P, BATCH], f32).ap()
    dense_part = nc.dram_tensor("dense_part", [STEPS, P, 8, MB], f32).ap()
    sums_v = sums.rearrange("(t p j) d -> t p (j d)", p=P, j=J)

    ctx = ExitStack()
    with ctx:
        def sb(name, shape, dt, c=ctx):
            return c.enter_context(nc.sbuf_tensor(name, shape, dt))

        def pb(name, shape, dt, c=ctx):
            return c.enter_context(nc.psum_tensor(name, shape, dt))

        def sem(name):
            return ctx.enter_context(nc.semaphore(name))

        ident = sb("ident", [P, P], f32)
        bias_sb = sb("bias_sb", [P, 22], f32)
        w4_sb = sb("w4_sb", [P, 2], f32)
        b4_sb = sb("b4_sb", [1, 1], f32)
        fetch_row = [sb(f"fetch_row{a}", [P, TABLES], i32) for a in range(2)]
        s_row = [sem(f"s_row{a}") for a in range(2)]
        s_bags = [sem(f"s_bags{b}") for b in range(2)]
        s_zero = [sem(f"s_zero{b}") for b in range(2)]
        with ExitStack() as tree:
            off_i = sb("off_i", [TABLES, BATCH], i32, tree)
            first = sb("first", [TABLES, BATCH], f32, tree)
            end = sb("end", [TABLES, BATCH], f32, tree)
            table_base = sb("table_base", [P, TABLES, J], f32, tree)
            idx_work = sb("idx_work", [P, TABLES, J], f32, tree)
            last_i = sb("last_i", [P, TILES, TABLES], i32, tree)
            start_i = sb("start_i", [P, TABLES, TILES], i32, tree)
            first_s = sb("first_s", [P, TABLES, TILES], f32, tree)
            end_s = sb("end_s", [P, TABLES, TILES], f32, tree)
            holds = sb("holds", [P, TABLES, TILES], f32, tree)
        w_hi = sb("w_hi", [P, CHUNKS, 1024], f32r)
        w_lo = sb("w_lo", [P, CHUNKS, 1024], f32r)

        with ExitStack() as one:
            rows = [sb(f"rows{u}", [P, J, D], f32, one) for u in range(2)]
            idx_now = [sb(f"idx_now{u}", [P, J], i32, one) for u in range(2)]
            idx_raw = sb("idx_raw", [P, TABLES, J], i32, one)
            start_hi = sb("start_hi", [P, TABLES, TILES], bf16, one)
            start_lo = sb("start_lo", [P, TABLES, TILES], bf16, one)
            last_base = sb("last_base", [P, TABLES], f32, one)
            column = sb("column", [P, P], f32, one)
            before = sb("before", [P, P], bf16, one)
            upto = sb("upto", [P, P], bf16, one)
            hot_p = sb("hot_p", [P, TILES, P], bf16, one)
            hot_j = sb("hot_j", [P, TILES, J], bf16, one)
            same = sb("same", [P, J], f32, one)
            begun = sb("begun", [P, J], f32, one)
            starts = sb("starts", [P, 1], f32, one)
            starts_b = sb("starts_b", [P, P], bf16, one)
            runs_upto = sb("runs_upto", [P, 1], f32, one)
            link_m = sb("link_m", [P, P], f32, one)
            xd = sb("xd", [DENSE, MB], f32, one)
            bw0_sb = sb("bw0_sb", [DENSE, BOT[0]], f32, one)
            bw1_sb = sb("bw1_sb", [P, 4, BOT[1]], f32, one)
            bw2_sb = sb("bw2_sb", [P, 2, BOT[2]], f32, one)
            bbias_sb = sb("bbias_sb", [P, 7], f32, one)
            hb0 = sb("hb0", [P, 4, MB], f32, one)
            hb1 = sb("hb1", [P, 2, MB], f32, one)
            xo = sb("xo", [P, MB], f32, one)
            part = [sb(f"part{u}", [P, MB], f32, one) for u in range(2)]
            w0x_sb = sb("w0x_sb", [P, TOP[0]], f32, one)
            w_raw = sb("w_raw", [P, 1024], f32, one)
            p_tr = [pb(f"p_tr{u}", [P, 16, TABLES], f32, one) for u in range(2)]
            p_start = pb("p_start", [P, J], f32, one)
            p_runs = pb("p_runs", [P, P + 1], f32, one)
            p_carry = pb("p_carry", [P, D], f32, one)
            p_mlp = pb("p_mlp", [P, 2, 512], f32, one)

            s_off, s_bw, s_w0 = sem("s_off"), sem("s_bw"), sem("s_w0")
            s_idx = [sem(f"s_idx{n}") for n in range(2)]
            s_ident, s_masks = sem("s_ident"), sem("s_masks")
            s_pool, s_starts_i = sem("s_pool"), sem("s_starts_i")
            s_chain = sem("s_chain")
            s_idxnow = [sem(f"s_idxnow{u}") for u in range(2)]
            s_rows = [[sem(f"s_rows{u}{c}") for c in range(QUARTERS)] for u in range(2)]
            s_summed = [sem(f"s_summed{u}") for u in range(2)]
            s_stored = [[sem(f"s_stored{u}{c}") for c in range(QUARTERS)] for u in range(2)]
            s_tree, s_trp, s_trc = sem("s_tree"), sem("s_trp"), sem("s_trc")
            s_last, s_lasto = sem("s_last"), sem("s_lasto")
            s_hot, s_hist, s_starts, s_runs, s_link, s_carry = (
                sem("s_hot"), sem("s_hist"), sem("s_starts"), sem("s_runs"), sem("s_link"), sem("s_carry"))
            s_scan, s_filling = sem("s_scan"), sem("s_filling")
            s_xd, s_mm, s_ev, s_xo = sem("s_xd"), sem("s_mm"), sem("s_ev"), sem("s_xo")
            s_part = [sem(f"s_part{u}") for u in range(2)]
            s_wraw, s_whi, s_wlo = sem("s_wraw"), sem("s_whi"), sem("s_wlo")

            block = one.enter_context(nc.Block())

            @block.sync
            def _(sp):
                idx_v = indices.rearrange("t (p j) -> p t j", j=J)
                for n, tables in enumerate((slice(0, 2), slice(2, TABLES))):
                    sp.dma_start(idx_raw[:, tables, :], idx_v[:, tables, :]).then_inc(s_idx[n], 16)
                sp.dma_start(off_i[:], offsets).then_inc(s_off, 16)
                sp.dma_start(bw0_sb[:], bw0).then_inc(s_bw, 16)
                sp.dma_start(bw1_sb[:], bw1.rearrange("(k p) o -> p k o", p=P)).then_inc(s_bw, 16)
                sp.dma_start(bw2_sb[:], bw2.rearrange("(k p) o -> p k o", p=P)).then_inc(s_bw, 16)
                sp.dma_start(bbias_sb[:], bbias).then_inc(s_bw, 16)
                sp.dma_start(bias_sb[:], tbias).then_inc(s_w0, 16)
                sp.dma_start(w4_sb[:], tw4).then_inc(s_w0, 16)
                sp.dma_start(b4_sb[:], tb4).then_inc(s_w0, 16)
                sp.dma_start(w0x_sb[:], tw0x).then_inc(s_w0, 16)
                sp.wait_ge(s_last, 1)
                sp.dma_start(last_row.rearrange("i p t -> p i t"), last_i[:]).then_inc(s_lasto, 16)
                sp.wait_ge(s_starts_i, 2)
                sp.wait_ge(s_lasto, 16)
                for a in range(2):
                    sp.dma_start(fetch_row[a][:], last_row[a, :, :]).then_inc(s_row[a], 16)

                def stores(r, u):
                    for c in range(QUARTERS):
                        sp.wait_ge(s_summed[u], r * QUARTERS + c + 1)
                        sp.dma_start(
                            sums_v[bass.ds(r * 2 + u, 1), :, bass.ts(c, JQ * D)].rearrange("a p n -> p (a n)"),
                            rows[u][:, bass.ts(c, JQ), :].rearrange("p j d -> p (j d)")
                        ).then_inc(s_stored[u][c], 16)

                def pair(r, mlp):
                    for u in range(2):
                        if mlp:
                            step = r * 2 + u
                            if not isinstance(step, int) or step > 0:
                                sp.wait_ge(s_wlo, step)
                            sp.dma_start(w_raw[:], tws[bass.ds(step * P, P), :]).then_inc(s_wraw, 16)
                            if not isinstance(step, int) or step > 0:
                                sp.wait_ge(s_mm, step * ND)
                            sp.dma_start(xd[:], dense_t[:, bass.ds(step * MB, MB)]).then_inc(s_xd, 16)
                        stores(r, u)

                pair(0, True)
                with sp.Fori(1, STEPS // 2) as r:
                    pair(r, True)
                with sp.Fori(STEPS // 2, TABLES // 2) as r:
                    pair(r, False)
                sp.wait_ge(s_xo, 16 * STEPS)
                for u in range(2):
                    sp.wait_ge(s_part[u], 16 * 4 * STEPS)
                sp.wait_ge(s_w0, 64)
                for u in range(2):
                    for c in range(QUARTERS):
                        sp.wait_ge(s_stored[u][c], 16 * (TABLES // 2))

            @block.gpsimd
            def _(pool):
                pool.iota(table_base[:], pattern=[[ROWS, TABLES], [0, J]], base=0, channel_multiplier=0,
                          allow_small_or_imprecise_dtypes=True).then_inc(s_pool, 1)
                pool.iota(last_base[:], pattern=[[BATCH, TABLES]], base=-1, channel_multiplier=0,
                          allow_small_or_imprecise_dtypes=True).then_inc(s_pool, 1)
                pool.iota(column[:], pattern=[[1, P]], base=0, channel_multiplier=0,
                          allow_small_or_imprecise_dtypes=True).then_inc(s_pool, 1)
                pool.memset(ident[:], 0.0).then_inc(s_ident, 1)
                pool.memset(before[:], 1.0).then_inc(s_ident, 1)
                pool.memset(upto[:], 1.0).then_inc(s_ident, 1)
                pool.wait_ge(s_ident, 3)
                pool.affine_select(out=ident[:], in_=ident[:], compare_op=ALU.not_equal, fill=1.0,
                                   base=0, pattern=[[-1, P]], channel_multiplier=1).then_inc(s_masks, 1)
                pool.affine_select(out=before[:], in_=before[:], compare_op=ALU.is_gt, fill=0.0,
                                   base=0, pattern=[[1, P]], channel_multiplier=-1).then_inc(s_masks, 1)
                pool.affine_select(out=upto[:], in_=upto[:], compare_op=ALU.is_ge, fill=0.0,
                                   base=0, pattern=[[1, P]], channel_multiplier=-1).then_inc(s_masks, 1)

                def gather(r, u):
                    pool.wait_ge(s_idxnow[u], r + 1)
                    for j in range(J):
                        if j % JQ == 0 and not isinstance(r, int):
                            pool.wait_ge(s_stored[u][j // JQ], r * 16)
                            pool.sem_inc(s_filling, 1)
                        pool.indirect_dma_start(
                            out=rows[u][:, j, :], out_offset=None, in_=emb,
                            in_offset=bass.IndirectOffsetOnAxis(ap=idx_now[u][:, j:j + 1], axis=0)
                        ).then_inc(s_rows[u][j // JQ], 16)

                gather(0, 0)
                gather(0, 1)
                with pool.Fori(1, TABLES // 2) as r:
                    gather(r, 0)
                    gather(r, 1)

                for c in range(QUARTERS):
                    pool.wait_ge(s_stored[0][c], 16 * (TABLES // 2))
                    pool.wait_ge(s_stored[1][c], 16 * (TABLES // 2 - 1))
                for b in range(2):
                    pool.memset(rows[0][:, HALF[0] * b:HALF[0] * b + HALF[b], :], 0.0).then_inc(s_zero[b], 1)
                pool.wait_ge(s_row[0], 16)
                for t in range(TABLES):
                    b = 0 if t < HALF[0] else 1
                    if t in (0, HALF[0]):
                        pool.wait_ge(s_zero[b], 1)
                    if t == TABLES - 1:
                        for c in range(QUARTERS):
                            pool.wait_ge(s_stored[1][c], 16 * (TABLES // 2))
                    pool.indirect_dma_start(
                        out=rows[0][:, t, :], out_offset=None, in_=sums[0:(t + 1) * BATCH, :],
                        in_offset=bass.IndirectOffsetOnAxis(ap=fetch_row[0][:, t:t + 1], axis=0),
                        bounds_check=(t + 1) * BATCH - 1, oob_is_err=False).then_inc(s_bags[b], 16)

            @block.scalar
            def _(act):
                def dense_step(t):
                    if not isinstance(t, int) or t > 0:
                        act.wait_ge(s_xo, t * 16)
                    for n in range(7):
                        dst = hb0[:, n, :] if n < 4 else hb1[:, n - 4, :] if n < 6 else xo[:]
                        act.wait_ge(s_mm, t * ND + n + 1)
                        nc.scalar.activation(dst, p_mlp[:, n % 2, 0:MB], ACT.Relu,
                                             bias=bbias_sb[:, n:n + 1]).then_inc(s_ev, 1)
                    act.wait_ge(s_ev, t * ND + 7)
                    act.dma_start(dense_out[:, bass.ds(t * MB, MB)], xo[:]).then_inc(s_xo, 16)
                    for o in range(8):
                        n, u = 7 + o, o % 2
                        act.wait_ge(s_mm, t * ND + n + 1)
                        if o >= 2 or not isinstance(t, int) or t > 0:
                            act.wait_ge(s_part[u], (t * 4 + o // 2) * 16)
                        nc.scalar.activation(part[u][:], p_mlp[:, n % 2, 0:MB], ACT.Identity,
                                             bias=bias_sb[:, o:o + 1]).then_inc(s_ev, 1)
                        act.wait_ge(s_ev, t * ND + n + 1)
                        act.dma_start(dense_part[bass.ds(t, 1), :, o, :].rearrange("a p n -> p (a n)"), part[u][:]
                                      ).then_inc(s_part[u], 16)

                def split_hi(t):
                    act.wait_ge(s_wraw, t * 16 + 16)
                    nc.scalar.activation(w_hi[:, bass.ds(t, 1), :].rearrange("p a n -> p (a n)"), w_raw[:],
                                         ACT.Copy).then_inc(s_whi, 1)

                act.wait_ge(s_bw, 64)
                act.wait_ge(s_w0, 64)
                split_hi(0)
                dense_step(0)
                with act.Fori(1, STEPS) as t:
                    split_hi(t)
                    dense_step(t)

            @block.vector
            def _(dve):
                chain = Chain(dve, s_chain)

                dve.wait_ge(s_pool, 3)
                for n, tables in enumerate((slice(0, 2), slice(2, TABLES))):
                    dve.wait_ge(s_idx[n], 16)
                    raw, work = idx_raw[:, tables, :], idx_work[:, tables, :]
                    chain.step(nc.vector.tensor_scalar(work, raw, 0.0, float(ROWS), ALU.is_lt, ALU.mult))
                    chain.step(nc.vector.tensor_tensor(work, work, raw, ALU.add))
                    chain.step(nc.vector.tensor_scalar(work, work, 0.0, float(ROWS - 1), ALU.max, ALU.min))
                    chain.step(nc.vector.tensor_tensor(raw, work, table_base[:, tables, :], ALU.add))
                    if n == 0:
                        for u in range(2):
                            nc.vector.tensor_copy(idx_now[u][:], idx_raw[:, u, :]).then_inc(s_idxnow[u], 1)

                chain.did(nc.vector.memset(first[:, 0:1], 0.0))
                chain.did(nc.vector.memset(end[:, 0:1], float(BATCH)))
                dve.wait_ge(s_off, 16)
                chain.settle()

                def every(t, start, step):
                    return t[:, start:BATCH:step]

                for level in range(TREE):
                    width = BATCH >> level
                    half = width // 2
                    chain.did(nc.vector.tensor_tensor(every(first, half, width), every(first, 0, width),
                                                      every(off_i, half, width), ALU.max))
                    chain.step(nc.vector.tensor_copy(every(end, half, width), every(end, 0, width)))
                    chain.step(nc.vector.tensor_tensor(every(end, 0, width), every(end, 0, width),
                                                       every(off_i, half, width), ALU.min))
                nc.vector.tensor_tensor(first[:, 0:1], first[:, 0:1], off_i[:, 0:1], ALU.max).then_inc(s_tree, 1)

                for n in range(4):
                    lo = 16 * (n // 2)
                    dve.wait_ge(s_trp, n + 1)
                    dst = (first_s, end_s)[n % 2]
                    nc.vector.tensor_copy(dst[:, :, lo:lo + 16].rearrange("p t i -> p i t"), p_tr[n % 2][:]
                                          ).then_inc(s_trc, 1)
                dve.wait_ge(s_trc, 4)
                chain.step(nc.vector.tensor_tensor(holds[:], end_s[:], first_s[:], ALU.is_gt))
                chain.did(nc.vector.scalar_tensor_tensor(first_s[:], first_s[:], float(-NONE), holds[:], ALU.add, ALU.mult))
                chain.step(nc.vector.scalar_tensor_tensor(end_s[:], end_s[:], float(-NONE), holds[:], ALU.add, ALU.mult))
                chain.step(nc.vector.tensor_scalar(start_i[:], first_s[:], float(NONE), None, ALU.add))
                nc.vector.scalar_tensor_tensor(last_i[:].rearrange("p i t -> p t i"), end_s[:], float(NONE),
                                               last_base[:].unsqueeze(2).to_broadcast([P, TABLES, TILES]),
                                               ALU.add, ALU.add).then_inc(s_last, 1)
                whole_i = idx_work[:].bitcast(i32)
                chain.step(nc.vector.tensor_scalar(whole_i, start_i[:], J.bit_length() - 1, None, ALU.arith_shift_right))
                nc.vector.tensor_copy(start_hi[:], whole_i).then_inc(s_starts_i, 1)
                chain.step(nc.vector.tensor_scalar(start_i[:], start_i[:], J - 1, None, ALU.bitwise_and))
                nc.vector.tensor_copy(start_lo[:], start_i[:]).then_inc(s_starts_i, 1)
                dve.wait_ge(s_starts_i, 2)

                def hot(t):
                    hi = start_hi[:, bass.ds(t, 1), :].rearrange("p a n -> p (a n)")
                    lo = start_lo[:, bass.ds(t, 1), :].rearrange("p a n -> p (a n)")
                    nc.vector.tensor_tensor(hot_p[:], hi.unsqueeze(2).to_broadcast([P, TILES, P]),
                                            column[:].unsqueeze(1).to_broadcast([P, TILES, P]),
                                            ALU.is_equal).then_inc(s_hot, 1)
                    nc.vector.tensor_tensor(hot_j[:], lo.unsqueeze(2).to_broadcast([P, TILES, J]),
                                            column[:, 0:J].unsqueeze(1).to_broadcast([P, TILES, J]),
                                            ALU.is_equal).then_inc(s_hot, 1)

                def runs(t):
                    dve.wait_ge(s_hist, t + 1)
                    chain.did(nc.vector.tensor_scalar(same[:], p_start[:], -1.0, 1.0, ALU.mult, ALU.add))
                    chain.step(nc.vector.reduce_sum(starts[:], p_start[:], AX.X))
                    nc.vector.tensor_copy(starts_b[:], starts[:].to_broadcast([P, P])).then_inc(s_starts, 1)
                    chain.did(nc.vector.tensor_tensor_scan(begun[:], same[:], same[:], 1.0, ALU.mult, ALU.mult))
                    dve.wait_ge(s_runs, t + 1)
                    chain.step(nc.vector.tensor_copy(runs_upto[:], p_runs[:, P:P + 1]))
                    nc.vector.scalar_tensor_tensor(link_m[:], p_runs[:, 0:P], runs_upto[:], before[:],
                                                   ALU.is_equal, ALU.mult).then_inc(s_link, 1)

                def table(r, u):
                    t = r * 2 + u
                    last_round = isinstance(r, int) and r == TABLES // 2 - 1
                    for j in range(1, J):
                        if j == 1 or j % JQ == 0:
                            dve.wait_ge(s_rows[u][j // JQ], (r + 1) * (16 * JQ))
                        if j == J - JQ and not last_round:
                            nc.vector.tensor_copy(idx_now[u][:],
                                                  idx_raw[:, bass.ds(t + 2, 1), :].rearrange("p a j -> p (a j)")
                                                  ).then_inc(s_idxnow[u], 1)
                        ins = nc.vector.scalar_tensor_tensor(rows[u][:, j, :], rows[u][:, j - 1, :], same[:, j:j + 1],
                                                             rows[u][:, j, :], ALU.mult, ALU.add)
                        if j < J - 1:
                            chain.step(ins)
                    ins.then_inc(s_scan, 1)
                    dve.wait_ge(s_carry, t + 1)
                    for j in range(J):
                        ins = nc.vector.scalar_tensor_tensor(rows[u][:, j, :], p_carry[:], begun[:, j:j + 1],
                                                             rows[u][:, j, :], ALU.mult, ALU.add)
                        if j % JQ == JQ - 1:
                            ins.then_inc(s_summed[u], 1)
                    if not (last_round and u == 1):
                        hot(t + 1)
                        dve.wait_ge(s_summed[u], (r + 1) * QUARTERS)
                        runs(t + 1)

                def split_lo(t):
                    dve.wait_ge(s_whi, t + 1)
                    nc.vector.tensor_tensor(w_lo[:, bass.ds(t, 1), :].rearrange("p a n -> p (a n)"), w_raw[:],
                                            w_hi[:, bass.ds(t, 1), :].rearrange("p a n -> p (a n)").bitcast(f32),
                                            ALU.subtract).then_inc(s_wlo, 1)

                hot(0)
                runs(0)
                chained = chain.n
                per_round = 2 * (J - 2 + 4)
                for start, stop in ((0, STEPS // 2), (STEPS // 2, TABLES // 2 - 1)):
                    with dve.Fori(start, stop) as r:
                        chain.round(r, per_round, chained)
                        for u in range(2):
                            table(r, u)
                            if start == 0:
                                split_lo(r * 2 + u)
                        assert chain.n == per_round
                chain.round(TABLES // 2 - 1, per_round, chained)
                for u in range(2):
                    table(TABLES // 2 - 1, u)

            @block.tensor
            def _(pe):
                pe.wait_ge(s_tree, 1)
                pe.wait_ge(s_masks, 3)
                for n in range(4):
                    if n >= 2:
                        pe.wait_ge(s_trc, n - 1)
                    src = first if n % 2 == 0 else end
                    for m in range(16):
                        i = 16 * (n // 2) + m
                        ins = nc.tensor.transpose(p_tr[n % 2][:, m, :], src[:, bass.ts(i, P)],
                                                  ident[0:TABLES, 0:TABLES])
                    ins.then_inc(s_trp, 1)

                def runs(t):
                    pe.wait_ge(s_hot, (t + 1) * 2)
                    for i in range(TILES):
                        ins = nc.tensor.matmul(p_start[:], hot_p[:, i, :], hot_j[:, i, :],
                                               start=(i == 0), stop=(i == TILES - 1))
                    ins.then_inc(s_hist, 1)
                    pe.wait_ge(s_starts, t + 1)
                    nc.tensor.matmul(p_runs[:, 0:P], starts_b[:], before[:], start=True, stop=True)
                    nc.tensor.matmul(p_runs[:, P:P + 1], upto[:], starts_b[:, 0:1], start=True, stop=True
                                     ).then_inc(s_runs, 1)

                def carry(t, u):
                    pe.wait_ge(s_link, t + 1)
                    pe.wait_ge(s_scan, t + 1)
                    nc.tensor.matmul(p_carry[:], link_m[:], rows[u][:, J - 1, :], start=True, stop=True
                                     ).then_inc(s_carry, 1)

                def dense_step(t, tiles):
                    if tiles[0] == 0:
                        pe.wait_ge(s_xd, t * 16 + 16)
                    for n in tiles:
                        bank = p_mlp[:, n % 2, 0:MB]
                        at = {0: 0, 1: 0, 4: 4, 5: 4, 6: 6, 7: 7}.get(n, n - 1)
                        if not isinstance(t, int) or t * ND + at > 0:
                            pe.wait_ge(s_ev, t * ND + at)
                        if n < 4:
                            ins = nc.tensor.matmul(bank, bw0_sb[:, bass.ts(n, P)], xd[:], start=True, stop=True)
                        elif n < 6:
                            for k in range(4):
                                ins = nc.tensor.matmul(bank, bw1_sb[:, k, bass.ts(n - 4, P)], hb0[:, k, :],
                                                       start=(k == 0), stop=(k == 3))
                        elif n < 7:
                            for k in range(2):
                                ins = nc.tensor.matmul(bank, bw2_sb[:, k, :], hb1[:, k, :],
                                                       start=(k == 0), stop=(k == 1))
                        else:
                            ins = nc.tensor.matmul(bank, w0x_sb[:, bass.ts(n - 7, P)], xo[:], start=True, stop=True)
                        ins.then_inc(s_mm, 1)

                def pair(r, mlp, last=False):
                    for u in range(2):
                        carry(r * 2 + u, u)
                        if mlp:
                            dense_step(r * 2 + u, range(7))
                        if not (last and u):
                            runs(r * 2 + u + 1)
                        if mlp:
                            dense_step(r * 2 + u, range(7, ND))

                runs(0)
                pe.wait_ge(s_bw, 64)
                pe.wait_ge(s_w0, 64)
                pair(0, True)
                with pe.Fori(1, STEPS // 2) as r:
                    pair(r, True)
                with pe.Fori(STEPS // 2, TABLES // 2 - 1) as r:
                    pair(r, False)
                pair(TABLES // 2 - 1, False, last=True)

        with ExitStack() as two:
            bags = [sb(f"bags{b}", [P, HALF[b], D], f32, two) for b in range(2)]
            feat_t = sb("feat_t", [P, P, 32], f32, two)
            dots = sb("dots", [P, NF, 32], f32, two)
            dots_t = sb("dots_t", [P, NF + SHIFTS, 32], f32, two)
            pairs = sb("pairs", [P, PAIRS], f32, two)
            dense_h = sb("dense_h", [P, 8, NB], f32, two)
            top_in = [sb(f"top_in_{part}", [P, 3, NB], f32r, two) for part in ("hi", "lo")]
            act_a = [sb(f"act_a_{part}", [P, 8, NB], f32r, two) for part in ("hi", "lo")]
            act_b = [sb(f"act_b_{part}", [P, 2, NB], f32r, two) for part in ("hi", "lo")]
            act_3 = sb("act_3", [P, 2, NB], f32, two)
            whole = [sb(f"whole{u}", [P, NB], f32, two) for u in range(2)]
            dense_in = sb("dense_in", [P, NB], f32, two)
            prob = sb("prob", [1, NB], f32, two)
            p_t = pb("p_t", [P, 2, 4, P], f32, two)
            p_z = pb("p_z", [P, 2, 512], f32, two)
            p_m = pb("p_m", [P, 2, 512], f32, two)
            p_acc = pb("p_acc", [P, 2, 2, NB], f32, two)

            s_fetching = sem("s_fetching")
            s_dense, s_part_in, s_featx, s_pad = sem("s_dense"), sem("s_part_in"), sem("s_featx"), sem("s_pad")
            s_t, s_tfree = sem("s_t"), sem("s_tfree")
            s_z, s_zact, s_zdve, s_zt, s_dt, s_pairs = (
                sem("s_z"), sem("s_zact"), sem("s_zdve"), sem("s_zt"), sem("s_dt"), sem("s_pairs"))
            s_r, s_rhi, s_rlo = sem("s_r"), sem("s_rhi"), sem("s_rlo")
            s_m, s_sum, s_mfree, s_acc, s_accfree = (
                sem("s_m"), sem("s_sum"), sem("s_mfree"), sem("s_acc"), sem("s_accfree"))
            s_hi, s_lo = sem("s_hi"), sem("s_lo")
            s_out = sem("s_out")

            NT, NZ = (TABLES + 3) // 4, P // 16
            mlp = [("M", 0, (o, 0)) for o in range(8)] + [("M", 1, (0, 0)), ("M", 1, (0, 1))]
            for o in range(1, 8):
                mlp += [("M", 1, (o, 0)), ("M", 1, (o, 1)), ("P", o - 1, None)]
            mlp += [("P", 7, None)] + [("M", 3, (o, k)) for k in range(4) for o in range(2)] + [("M", 4, (0, 0))]
            STEADY = (("T", 0, (-9, -9, -1, 0, 3, 5, 6)), ("Z", 0, (8, 9, 10, 11, 12, 13, 14, 15)),
                      ("T", 1, (16, 17, 18, 19, 20, 21, 22)), ("R", 0, (20,)),
                      ("Z", 1, (23, 24, 25, 26, 27, 28, 29, 30)), ("R", 1, (38,)))
            FIRST = (("T", 0, (-9, -9, -1, 10, 11, 12, 13)), ("Z", 0, (14, 15, 15, 16, 16, 17, 17, 18)),
                     ("T", 1, (18, 19, 20, 22, 23, 23, 24)), ("R", 0, (23,)),
                     ("Z", 1, (25, 26, 27, 27, 28, 29, 30, 30)), ("R", 1, (39,)))
            LEAD = {(kind, a, c): 2 if slot < 0 else 1 for kind, a, slots in STEADY for c, slot in enumerate(slots)}

            def order_of(plan):
                ahead = {slot: [] for slot in range(len(mlp))}
                for kind, a, slots in plan:
                    for c, slot in enumerate(slots):
                        ahead[slot % len(mlp)].append((kind, a, c))
                return [step for slot, m in enumerate(mlp) for step in ahead[slot] + [m]]

            steady, first_order = order_of(STEADY), order_of(FIRST)
            NM = 19
            BANK_M = [m % 2 for m in range(NM - 1)] + [(NM - 2) % 2]
            LAST_IN_M = [NM - 3, NM - 1] + list(range(NM - 3)) + [NM - 2]
            M_BEFORE = (0, 8, None, 16, 18)
            K_TILES = (3, 8, None, 4, 2)
            PARTS = (1, 2, None, 4, 1)
            ring = [step for step in steady if step[0] in "TR"]
            BANK = {step: n % 2 for n, step in enumerate(ring)}
            LAST_IN_BANK = {step: (ring[n - 2], LEAD[step] - LEAD[ring[n - 2]] + (0 if n >= 2 else 1))
                            for n, step in enumerate(ring)}
            NS = 20

            def steps(handlers, g, order=steady):
                for kind, x, y in order:
                    group = g + LEAD.get((kind, x, y), 0)
                    if not isinstance(g, int) or 0 <= group < GROUPS:
                        handlers[kind](group, x, y)

            def rounds(engine, handlers):
                steps(handlers, -2)
                steps(handlers, -1)
                steps(handlers, 0, first_order)
                with engine.Fori(1, GROUPS - 2) as g:
                    steps(handlers, g)
                for g in (GROUPS - 2, GROUPS - 1):
                    steps(handlers, g)

            def wait(engine, semaphore, value):
                if not isinstance(value, int) or value > 0:
                    engine.wait_ge(semaphore, value)

            def tables_of(c):
                return range(4 * c, min(4 * c + 4, TABLES))

            block = two.enter_context(nc.Block())

            @block.sync
            def _(sp):
                def inputs(g):
                    tile = g * 2 if isinstance(g, int) else sp.snap(g * 2)
                    for a in range(2):
                        if not isinstance(g, int) or g > 0:
                            sp.wait_ge(s_t, (tile + (a - 1)) * NT)
                            sp.dma_start(fetch_row[a][:],
                                         last_row[bass.ds(tile + a, 1), :, :].rearrange("a p t -> p (a t)")
                                         ).then_inc(s_row[a], 16)
                        if a == 0:
                            wait(sp, s_featx, g * 2)
                            sp.dma_start(dense_in[:], dense_out[:, bass.ds(g * NB, NB)]).then_inc(s_dense, 16)

                def dense_parts(g):
                    wait(sp, s_sum, g * 8)
                    sp.dma_start(dense_h[:].rearrange("p o n -> p (o n)"),
                                 dense_part[bass.ds(g, 1), :, :, :].rearrange("a p o n -> p (a o n)")
                                 ).then_inc(s_part_in, 16)

                inputs(0)
                inputs(1)
                dense_parts(0)
                with sp.Fori(2, GROUPS) as g:
                    dense_parts(g - 1)
                    inputs(g)
                dense_parts(GROUPS - 1)

            @block.gpsimd
            def _(pool):
                def fetch(g, a):
                    pool.wait_ge(s_row[a], (g + 1) * 16)
                    for b in range(2):
                        pool.wait_ge(s_zero[b], g * 2 + (a + 1))
                        if not isinstance(g, int):
                            pool.sem_inc(s_fetching, 1)
                        for n in range(HALF[b]):
                            t = HALF[0] * b + n
                            pool.indirect_dma_start(
                                out=bags[b][:, n, :], out_offset=None, in_=sums,
                                in_offset=bass.IndirectOffsetOnAxis(ap=fetch_row[a][:, t:t + 1], axis=0),
                                bounds_check=TABLES * BATCH - 1, oob_is_err=False).then_inc(s_bags[b], 16)

                fetch(0, 1)
                with pool.Fori(1, GROUPS) as g:
                    fetch(g, 0)
                    fetch(g, 1)

            @block.tensor
            def _(pe):
                def bank_free(g, step):
                    (kind, a, c), back = LAST_IN_BANK[step]
                    while isinstance(g, int) and g - back >= GROUPS:
                        g -= back
                        (kind, a, c), back = LAST_IN_BANK[kind, a, c]
                    if kind == "T":
                        wait(pe, s_tfree, (g - back) * (2 * NT) + (a * NT + c + 1))
                    else:
                        wait(pe, s_rlo, (g - back) * 2 + (a + 1))

                def transposes(g, a, c):
                    i = g * 2 + a
                    if c in (0, 3):
                        pe.wait_ge(s_bags[c // 3], (i + 1) * (16 * HALF[c // 3]))
                    bank_free(g, ("T", a, c))
                    for n, t in enumerate(tables_of(c)):
                        b = 0 if t < HALF[0] else 1
                        ins = nc.tensor.transpose(p_t[:, BANK["T", a, c], n, :], bags[b][:, t - HALF[0] * b, :],
                                                  ident[:])
                    ins.then_inc(s_t, 1)

                def dot(g, a, c):
                    if c == 0:
                        pe.wait_ge(s_tfree, g * (2 * NT) + (a + 1) * NT)
                        pe.wait_ge(s_featx, g * 2 + a + 1)
                    wait(pe, s_zact, g * (2 * NZ) + a * NZ + c - 1)
                    wait(pe, s_zdve, g * (2 * NZ) + a * NZ + c - 1)
                    for n in range(4):
                        four = feat_t[:, bass.ts(4 * c + n, 4), :]
                        ins = nc.tensor.matmul(p_z[:, c % 2, bass.ts(n, 4 * NF)],
                                               four.rearrange("p i f -> p (i f)"), four[:, :, 0:NF],
                                               start=True, stop=True)
                    ins.then_inc(s_z, 1)

                def pair_transposes(g, a, _):
                    pe.wait_ge(s_pairs, g * 2 + a + 1)
                    bank_free(g, ("R", a, 0))
                    for n in range(3):
                        width = min(P, PAIRS - n * P)
                        ins = nc.tensor.transpose(p_t[0:width, BANK["R", a, 0], n, :], pairs[:, n * P:n * P + width], ident[:])
                    ins.then_inc(s_r, 1)

                def in_parts(out_ap, w, x, start, stop, shared=False):
                    nc.tensor.matmul(out_ap, w[0], x[0], start=start, stop=False, skip_group_check=shared)
                    nc.tensor.matmul(out_ap, w[0], x[1], start=False, stop=False, skip_group_check=shared)
                    return nc.tensor.matmul(out_ap, w[1], x[0], start=False, stop=stop, skip_group_check=shared)

                def product(g, layer, tile_part):
                    o, part = tile_part
                    m = M_BEFORE[layer] + o
                    bank = p_m[0:1 if layer == 4 else P, BANK_M[m], 0:NB]
                    if part == 0:
                        last = LAST_IN_M[m]
                        at = g - 1 if m < 2 else g
                        if last < 8:
                            wait(pe, s_sum, at * 8 + last + 1)
                        else:
                            wait(pe, s_mfree, at * (NM - 8) + (last - 7))
                    if layer == 0 and o == 0:
                        pe.wait_ge(s_rlo, g * 2 + 2)
                    K = K_TILES[layer]
                    for k in range(part * K // PARTS[layer], (part + 1) * K // PARTS[layer]):
                        if o == 0 and layer == 1:
                            pe.wait_ge(s_lo, g * NS + k + 1)
                        if o == 0 and layer == 3:
                            pe.wait_ge(s_lo, g * NS + 16 + k + 1)
                        if layer == 4 and k == 0:
                            pe.wait_ge(s_mfree, g * (NM - 8) + NM - 9)
                        if layer == 4:
                            ins = nc.tensor.matmul(bank, w4_sb[:, k:k + 1], act_3[:, k, :],
                                                   start=(k == 0), stop=(k == K - 1))
                            continue
                        height = SHORT if layer == 0 and k == 2 else P
                        chunk, at = {0: (PAIR_CHUNK + k, o * P), 1: (k, o * P), 3: (12, k * TOP[3] + o * P)}[layer]
                        x = top_in if layer == 0 else act_a
                        ins = in_parts(bank, [w[0:height, chunk, at:at + P] for w in (w_hi, w_lo)],
                                       [half[0:height, k, :] for half in x], k == 0, k == K - 1)
                    if k == K - 1:
                        ins.then_inc(s_m, 1)

                def layer_2(g, k, _):
                    pe.wait_ge(s_lo, g * NS + 8 + k + 1)
                    if k == 0:
                        wait(pe, s_accfree, g * 4)
                    for o in range(4):
                        at = (k % 2) * TOP[2] + o * P
                        ins = in_parts(p_acc[:, o // 2, o % 2, :], [w[:, 8 + k // 2, at:at + P] for w in (w_hi, w_lo)],
                                       [half[:, k % 2, :] for half in act_b], k == 0 and o % 2 == 0, k == 7, True)
                        if k == 7:
                            ins.then_inc(s_acc, 1)

                pe.wait_ge(s_pad, 1)
                rounds(pe, {"T": transposes, "Z": dot, "R": pair_transposes, "M": product, "P": layer_2})

            def drop_dots(engine_copy, g, a, c, side):
                for i in (2 * side, 2 * side + 1):
                    ins = engine_copy(
                        view(dots, 4 * c, [[1, 4], [32, NF]], 32, 32 * i),
                        view(p_z, 512 * (c % 2) + i * NF, [[4 * NF, 4], [1, NF]], 32, 32 * i))
                return ins

            @block.scalar
            def _(act):
                def features(g, a, c):
                    n = len(tables_of(c))
                    act.wait_ge(s_t, g * (2 * NT) + a * NT + c + 1)
                    if c == 0:
                        wait(act, s_z, g * (2 * NZ) + a * NZ)
                    nc.scalar.activation(
                        view(feat_t, 1 + 4 * c, [[1, n], [32, 4], [P, 32]]),
                        p_t[:, BANK["T", a, c], 0:n, :].rearrange("p n (i s) -> p n i s", i=4),
                        ACT.Copy).then_inc(s_tfree, 1)

                def dots_out(g, a, c):
                    act.wait_ge(s_z, g * (2 * NZ) + a * NZ + c + 1)
                    if c == 0:
                        wait(act, s_zt, g * 2 + a)
                    drop_dots(lambda o, i: nc.scalar.activation(o, i, ACT.Copy), g, a, c, 0).then_inc(s_zact, 1)

                def pairs_hi(g, a, _):
                    act.wait_ge(s_r, g * 2 + a + 1)
                    wait(act, s_m, (g - 1) * NM + 8)
                    bank = BANK["R", a, 0]
                    nc.scalar.activation(top_in[0][:, 0:2, bass.ts(a, P)], p_t[:, bank, 0:2, :], ACT.Copy)
                    nc.scalar.activation(top_in[0][0:SHORT, 2, bass.ts(a, P)], p_t[0:SHORT, bank, 2, :], ACT.Copy
                                         ).then_inc(s_rhi, 1)

                def layer_out(g, layer, tile_part):
                    o, part = tile_part
                    if part < PARTS[layer] - 1:
                        return
                    m = M_BEFORE[layer] + o
                    if layer == 0:
                        act.wait_ge(s_sum, g * 8 + o + 1)
                        nc.scalar.activation(act_a[0][:, o, :], whole[o % 2][:], ACT.Relu).then_inc(s_hi, 1)
                        return
                    act.wait_ge(s_m, g * NM + m + 1)
                    bank = p_m[:, BANK_M[m], 0:NB]
                    if layer == 1:
                        split_out(g, bank, bias_sb[:, 8 + o:9 + o], act_b[0][:, o % 2, :], 8 + o, s_mfree)
                    elif layer == 3:
                        nc.scalar.activation(act_3[:, o, :], bank, ACT.Relu, bias=bias_sb[:, 20 + o:21 + o]
                                             ).then_inc(s_mfree, 1)
                    else:
                        wait(act, s_out, g * 16)
                        nc.scalar.activation(prob[:], bank[0:1, :], ACT.Sigmoid, bias=b4_sb[:]).then_inc(s_mfree, 1)
                        act.wait_ge(s_mfree, (g + 1) * (NM - 8))
                        act.dma_start(out[bass.ds(g * NB, NB), :].rearrange("b a -> a b"), prob[:]).then_inc(s_out, 16)

                def split_out(g, bank, bias, hi, n, free):
                    wait(act, s_lo, g * NS + n - 1)
                    nc.scalar.activation(whole[n % 2][:], bank, ACT.Relu, bias=bias)
                    nc.scalar.activation(hi, bank, ACT.Relu, bias=bias).then_inc(free, 1)

                def layer_2_out(g, k, _):
                    if k < 7:
                        return
                    for o in range(4):
                        act.wait_ge(s_acc, g * 4 + 2 * (o // 2) + 2)
                        split_out(g, p_acc[:, o // 2, o % 2, :], bias_sb[:, 16 + o:17 + o], act_a[0][:, o, :],
                                  16 + o, s_accfree)

                rounds(act, {"T": features, "Z": dots_out, "R": pairs_hi, "M": layer_out, "P": layer_2_out})
                act.wait_ge(s_out, 16 * GROUPS)

            @block.vector
            def _(dve):
                def empty(g, a, b):
                    dve.wait_ge(s_t, g * (2 * NT) + a * NT + (3, NT)[b])
                    nc.vector.memset(bags[b][:], 0.0).then_inc(s_zero[b], 1)

                def features(g, a, c):
                    if c == 0:
                        if a == 0:
                            dve.wait_ge(s_dense, g * 16 + 16)
                        wait(dve, s_z, g * (2 * NZ) + a * NZ)
                        nc.vector.tensor_copy(view(feat_t, 0, [[32, 4], [P, 32]]),
                                              dense_in[:, bass.ts(a, P)].rearrange("p (i s) -> p i s", i=4)
                                              ).then_inc(s_featx, 1)
                    if c == 2 or (a, c) == (1, NT - 1):
                        empty(g, a, 0 if c == 2 else 1)

                def dots_out(g, a, c):
                    dve.wait_ge(s_z, g * (2 * NZ) + a * NZ + c + 1)
                    if c == 0:
                        wait(dve, s_zt, g * 2 + a)
                    drop_dots(nc.vector.tensor_copy, g, a, c, 1).then_inc(s_zdve, 1)
                    if (a, c) == (0, 1):
                        empty(g, a, 1)
                    if c == NZ - 1:
                        n = g * 2 + a + 1
                        dve.wait_ge(s_zact, g * (2 * NZ) + (a + 1) * NZ)
                        dve.wait_ge(s_zdve, g * (2 * NZ) + (a + 1) * NZ)
                        nc.vector.transpose(dots_t[:, 0:NF, :].rearrange("p m n -> p (m n)"),
                                            dots[:].rearrange("p m s -> p (m s)")).then_inc(s_zt, 1)
                        dve.wait_ge(s_zt, n)
                        nc.vector.tensor_copy(dots_t[:, NF:NF + SHIFTS, :], dots_t[:, 0:SHIFTS, :]).then_inc(s_dt, 1)
                        dve.wait_ge(s_dt, n)
                        wait(dve, s_r, n - 1)
                        nc.vector.tensor_copy(pairs[:].rearrange("p (k n) -> p k n", n=NF),
                                              view(dots_t, 32, [[32, SHIFTS], [33, NF]])).then_inc(s_pairs, 1)

                def pairs_lo(g, a, _):
                    bank = BANK["R", a, 0]
                    dve.wait_ge(s_rhi, g * 2 + a + 1)
                    nc.vector.tensor_tensor(top_in[1][:, 0:2, bass.ts(a, P)], p_t[:, bank, 0:2, :],
                                            top_in[0][:, 0:2, bass.ts(a, P)].bitcast(f32), ALU.subtract)
                    nc.vector.tensor_tensor(top_in[1][0:SHORT, 2, bass.ts(a, P)], p_t[0:SHORT, bank, 2, :],
                                            top_in[0][0:SHORT, 2, bass.ts(a, P)].bitcast(f32), ALU.subtract
                                            ).then_inc(s_rlo, 1)

                def lower(lo, hi, n):
                    nc.vector.tensor_tensor(lo, whole[n % 2][:], hi.bitcast(f32), ALU.subtract).then_inc(s_lo, 1)

                def layer_0_lower(g, o):
                    dve.wait_ge(s_hi, g * 8 + o + 1)
                    nc.vector.scalar_tensor_tensor(act_a[1][:, o, :], whole[o % 2][:], 0.0,
                                                   act_a[0][:, o, :].bitcast(f32), ALU.max, ALU.subtract
                                                   ).then_inc(s_lo, 1)

                def layer_out(g, layer, tile_part):
                    o, part = tile_part
                    if layer == 0:
                        if o == 0:
                            dve.wait_ge(s_part_in, g * 16 + 16)
                        dve.wait_ge(s_m, g * NM + o + 1)
                        wait(dve, s_lo, g * NS + o - 1)
                        nc.vector.tensor_tensor(whole[o % 2][:], p_m[:, o % 2, 0:NB], dense_h[:, o, :], ALU.add
                                                ).then_inc(s_sum, 1)
                        if o > 0:
                            layer_0_lower(g, o - 1)
                        if o == 7:
                            layer_0_lower(g, o)
                    elif layer == 1 and part == 1:
                        dve.wait_ge(s_mfree, g * (NM - 8) + o + 1)
                        lower(act_b[1][:, o % 2, :], act_b[0][:, o % 2, :], 8 + o)

                def layer_2_out(g, k, _):
                    if k == 7:
                        for o in range(4):
                            dve.wait_ge(s_accfree, g * 4 + o + 1)
                            lower(act_a[1][:, o, :], act_a[0][:, o, :], 16 + o)

                nc.vector.memset(feat_t[:, :, NF:32], 0.0).then_inc(s_pad, 1)
                rounds(dve, {"T": features, "Z": dots_out, "R": pairs_lo, "M": layer_out, "P": layer_2_out})



def kernel(r_lS_o, r_lS_i, L0_rec_dense_x, L0_rec_emb_w,
           L0_rec_bot_w0, L0_rec_bot_b0, L0_rec_bot_w1, L0_rec_bot_b1, L0_rec_bot_w2, L0_rec_bot_b2,
           L0_rec_top_w0, L0_rec_top_b0, L0_rec_top_w1, L0_rec_top_b1, L0_rec_top_w2, L0_rec_top_b2,
           L0_rec_top_w3, L0_rec_top_b3, L0_rec_top_w4, L0_rec_top_b4):
    import concourse.bacc as bacc
    from concourse.bass_utils import run_bass_kernel_spmd

    def cols(*biases):
        return np.concatenate([np.reshape(b, (-1, P)).T for b in biases], axis=1)

    order = []
    for k in range(1, SHIFTS + 1):
        for n in range(NF):
            hi, lo = max(n, (n + k) % NF), min(n, (n + k) % NF)
            order.append(P + hi * (hi - 1) // 2 + lo)
    w0, w1, w2, w3 = (np.asarray(w) for w in (L0_rec_top_w0, L0_rec_top_w1, L0_rec_top_w2, L0_rec_top_w3))
    chunks = np.concatenate([
        w1.T,
        w2.T.reshape(4, 2, P, TOP[2]).transpose(0, 2, 1, 3).reshape(4 * P, CHUNK),
        w3.T.reshape(4, P, TOP[3]).transpose(1, 0, 2).reshape(P, CHUNK),
        w0.T[order + order[-SHORT:][:P - SHORT]],
    ])
    arrays = {
        "offsets": np.asarray(r_lS_o),
        "indices": np.asarray(r_lS_i),
        "dense_t": np.asarray(L0_rec_dense_x).T,
        "emb": np.reshape(L0_rec_emb_w, (TABLES * ROWS, D)),
        "bw0": np.asarray(L0_rec_bot_w0).T,
        "bw1": np.asarray(L0_rec_bot_w1).T,
        "bw2": np.asarray(L0_rec_bot_w2).T,
        "bbias": cols(L0_rec_bot_b0, L0_rec_bot_b1, L0_rec_bot_b2),
        "tw0x": w0.T[:P],
        "tws": chunks,
        "tw4": cols(L0_rec_top_w4),
        "tbias": cols(L0_rec_top_b0, L0_rec_top_b1, L0_rec_top_b2, L0_rec_top_b3),
        "tb4": np.reshape(L0_rec_top_b4, (1, 1)),
    }
    arrays = {name: np.ascontiguousarray(a) for name, a in arrays.items()}
    nc = bacc.Bacc("TRN2", target_bir_lowering=False, num_devices=1)
    args = [nc.dram_tensor(name, a.shape, mybir.dt.from_np(a.dtype), kind="ExternalInput").ap()
            for name, a in arrays.items()]
    out = nc.dram_tensor("out", (BATCH, 1), mybir.dt.float32, kind="ExternalOutput").ap()
    rec_kernel(nc, *args, out)
    r = run_bass_kernel_spmd(nc, [arrays], core_ids=[0])
    return r.results[0]["out"]
```
